# Optimizing a Trainium2 kernel written in Bass

```python
import numpy as np
import jax
import jax.numpy as jnp

def _softmax(x, axis=-1):
    return jax.nn.softmax(x, axis=axis)
def _gelu(x):
    return jax.nn.gelu(x, approximate=True)
def _silu(x):
    return jax.nn.silu(x)
def _sigmoid(x):
    return jax.nn.sigmoid(x)
def _layernorm(x, axis=-1, eps=1e-5):
    m = jnp.mean(x, axis=axis, keepdims=True)
    v = jnp.var(x, axis=axis, keepdims=True)
    return (x - m) / jnp.sqrt(v + eps)
def _scatter_add(tgt, idx, src, axis=0):
    return tgt.at[idx].add(src)
def _segment_sum(src, seg, n):
    return jax.ops.segment_sum(src, seg, n)

kernel_name = 'mk_conv_seq_d1_conv_nchw256_9dba5c'

def setup_inputs(seed: int = 0):
    np.random.seed(seed)
    _w = jnp.asarray
    def _rec_inputs():
        import jax
        import jax.numpy as jnp
        _gk = jax.random.key(seed)
        x = 7.22e-05 + 1 * jax.random.normal(jax.random.fold_in(_gk, 1), (8, 256, 64, 64), jnp.float32)
        return x
    x = _rec_inputs()
    def _L0_conv_setup():
        import jax, jax.numpy as jnp
        import numpy as np
        B, C, H, W = (8, 256, 64, 64)
        S = 2
        A = S * S
        NH = 8
        EPS = 1e-05
        key = jax.random.key(seed)
        ks = jax.random.split(key, 4)
        scale = 0.02
        return {'x': jax.random.normal(ks[0], (B, C, H, W), jnp.float32), 'W_in': jax.random.normal(ks[1], (A, 3 * C, C), jnp.float32) * scale, 'b_in': jnp.zeros((A, 3 * C), jnp.float32), 'W_out': jax.random.normal(ks[2], (A, C, C), jnp.float32) * scale, 'b_out': jnp.zeros((A, C), jnp.float32), 'gamma': jnp.ones((C,), jnp.float32), 'beta': jnp.zeros((C,), jnp.float32)}
    _L0_conv_all = _L0_conv_setup()
    _L0_conv_in = {k: v for k, v in _L0_conv_all.items() if k in ('W_in', 'b_in', 'W_out', 'b_out', 'gamma', 'beta', )}
    del _L0_conv_all

    return {
        "x": x,
        "L0_conv_W_in": _L0_conv_in["W_in"],
        "L0_conv_b_in": _L0_conv_in["b_in"],
        "L0_conv_W_out": _L0_conv_in["W_out"],
        "L0_conv_b_out": _L0_conv_in["b_out"],
        "L0_conv_gamma": _L0_conv_in["gamma"],
        "L0_conv_beta": _L0_conv_in["beta"],
    }

def reference(x, L0_conv_W_in, L0_conv_b_in, L0_conv_W_out, L0_conv_b_out, L0_conv_gamma, L0_conv_beta):
    import jax
    import jax.numpy as jnp
    def _L0_conv_ref(x, W_in, b_in, W_out, b_out, gamma, beta):
        import jax, jax.numpy as jnp
        import numpy as np
        B, C, H, W = (8, 256, 64, 64)
        S = 2
        A = S * S
        NH = 8
        EPS = 1e-05
        b, c, h, w = x.shape
        ah, aw = (h // S, w // S)
        L = ah * aw
        dh = c // NH
        xa = x.reshape(b, c, S, ah, S, aw).transpose(0, 2, 4, 3, 5, 1).reshape(b, A, L, c)
        qkv = jnp.einsum('balc,adc->bald', xa, W_in) + b_in[None, :, None, :]
        q, k, v = jnp.split(qkv, 3, axis=-1)
        q = q.reshape(b, A, L, NH, dh)
        k = k.reshape(b, A, L, NH, dh)
        v = v.reshape(b, A, L, NH, dh)
        scale = jnp.asarray(dh, x.dtype) ** (-0.5)
        scores = jnp.einsum('balhd,bamhd->bahlm', q * scale, k)
        attn = jax.nn.softmax(scores, axis=-1)
        o = jnp.einsum('bahlm,bamhd->balhd', attn, v).reshape(b, A, L, c)
        o = jnp.einsum('balc,adc->bald', o, W_out) + b_out[None, :, None, :]
        y = o + xa
        mu = jnp.mean(y, axis=-1, keepdims=True)
        var = jnp.mean((y - mu) ** 2, axis=-1, keepdims=True)
        y = (y - mu) * jax.lax.rsqrt(var + EPS) * gamma + beta
        out = y.reshape(b, S, S, ah, aw, c).transpose(0, 5, 1, 3, 2, 4).reshape(b, c, h, w)
        return out

    def _gn(v, G=32, eps=1e-5):
        B_, C_, H_, W_ = v.shape
        g = v.reshape(B_, G, C_ // G, H_, W_)
        m = jnp.mean(g, axis=(2, 3, 4), keepdims=True)
        s = jnp.var(g, axis=(2, 3, 4), keepdims=True)
        return ((g - m) / jnp.sqrt(s + eps)).reshape(v.shape)

    def _ln_c(v, eps=1e-6):
        m = jnp.mean(v, axis=1, keepdims=True)
        s = jnp.var(v, axis=1, keepdims=True)
        return (v - m) / jnp.sqrt(s + eps)

    def _ln_t(v, eps=1e-5):
        m = jnp.mean(v, axis=-1, keepdims=True)
        s = jnp.var(v, axis=-1, keepdims=True)
        return (v - m) / jnp.sqrt(s + eps)

    def _to_tokens(v):
        B_, C_, H_, W_ = v.shape
        return v.reshape(B_, C_, H_ * W_).transpose(0, 2, 1)
    def _from_tokens(t, like):
        B_, C_, H_, W_ = like.shape
        return t.transpose(0, 2, 1).reshape(B_, C_, H_, W_)

    x = _L0_conv_ref(x, L0_conv_W_in, L0_conv_b_in, L0_conv_W_out, L0_conv_b_out, L0_conv_gamma, L0_conv_beta)
    return x


_drawn_inputs = setup_inputs


def setup_inputs(seed=0):
    import zlib

    import numpy as np

    out = dict(_drawn_inputs(seed))
    spreads = {'L0_conv_b_in': (0.0, 0.1),
     'L0_conv_b_out': (0.0, 0.1),
     'L0_conv_gamma': (1.0, 0.2),
     'L0_conv_beta': (0.0, 0.1)}
    factors = {'L0_conv_W_in': 8.0}
    for name, (base, spread) in spreads.items():
        noise = np.random.default_rng([zlib.crc32(name.encode()), seed]).standard_normal(out[name].shape)
        drawn = base * np.exp(spread * noise) if base else spread * noise
        out[name] = jnp.asarray(drawn.astype(out[name].dtype))
    for name, factor in factors.items():
        out[name] = (out[name] * factor).astype(out[name].dtype)
    return out
```

```python
from contextlib import ExitStack

import concourse.bass as bass
from concourse import mybir

F32 = mybir.dt.float32
F32R = mybir.dt.float32r
ALU = mybir.AluOpType
ACT = mybir.ActivationFunctionType

BATCH, CHANNELS, HEIGHT, WIDTH = 8, 256, 64, 64
SPLIT = 2
AREAS = SPLIT * SPLIT
HEADS = 8
DH = CHANNELS // HEADS
TOKENS = HEIGHT * WIDTH // AREAS
PAIRS = AREAS * BATCH
EPS = 1e-5
SCALE = float(DH) ** -0.5

P = 128
CT = CHANNELS // P
HALF = TOKENS // 2
HPS = 2
STEPS = HEADS // HPS
KEYS = TOKENS // P
SLOTS = STEPS * KEYS
LEAD = 2
GROUPS = 8
PRING = 4
QROWS = 3 * DH
CROWS = 2
ROWS = QROWS + CROWS
PIECE = 128


class Pair:

    def __init__(self, reg, off):
        self.reg, self.off = reg, off

    def at(self, n, k):
        return self.off * n + k if self.reg is None else self.reg * (2 * n) + (self.off * n + k)

    def plus(self, k):
        return Pair(self.reg, self.off + k)

    def number(self):
        return self.off if self.reg is None else self.reg * 2 + self.off


LAST, CUR, NEXT = "last", "cur", "next"
FILL = [
    (2, "rowsum", 3, LAST),
    (5, "outproj", 0, LAST), (6, "outproj", 1, LAST), (6, "maxrow", 1, CUR),
    (7, "outproj", 2, LAST), (8, "outproj", 3, LAST),
    (9, "mean", 0, LAST), (10, "rowsum", 0, CUR), (11, "mean", 1, LAST),
    (12, "var", 0, LAST), (13, "var", 1, LAST),
    (14, "qk", 0, NEXT), (14, "maxrow", 2, CUR), (15, "qk", 1, NEXT), (16, "qk", 2, NEXT),
    (17, "qk", 3, NEXT), (18, "rowsum", 1, CUR),
    (19, "v", 0, NEXT), (20, "v", 1, NEXT), (21, "v", 2, NEXT), (22, "v", 3, NEXT),
    (22, "maxrow", 3, CUR),
    (23, "qk", 4, NEXT), (24, "qk", 5, NEXT), (25, "qk", 6, NEXT), (26, "rowsum", 2, CUR),
    (27, "qk", 7, NEXT), (30, "maxrow", 0, NEXT),
]


def fills(has):
    return [f for f in FILL if f[3] in has]


class Turn:

    def __init__(self, pair, parity, has):
        self.pair, self.parity, self.has = pair, parity, has
        self.fill = fills(has)

    def filled(self, kind, index):
        n = [(k, i) for _, k, i, _ in self.fill].index((kind, index))
        first = len(fills((NEXT,)))
        second = first + len(fills((CUR, NEXT)))
        full = len(FILL)
        if self.pair.reg is None:
            p = self.pair.off
            if p < 0:
                return n
            if p == 0:
                return first + n
            if p == PAIRS:
                return second + (PAIRS - 2) * full + len(fills((LAST, CUR))) + n
        return self.pair.at(full, second - full + n)

    def whose(self, name):
        return self.pair.plus({LAST: -1, CUR: 0, NEXT: 1}[name])


def turns(engine, emit):
    emit(Turn(Pair(None, -1), 1, (NEXT,)))
    emit(Turn(Pair(None, 0), 0, (CUR, NEXT)))
    with engine.Fori(0, PAIRS // 2 - 1) as i:
        emit(Turn(Pair(i, 1), 1, (LAST, CUR, NEXT)))
        emit(Turn(Pair(i, 2), 0, (LAST, CUR, NEXT)))
    emit(Turn(Pair(None, PAIRS - 1), 1, (LAST, CUR)))
    emit(Turn(Pair(None, PAIRS), 0, (LAST,)))


def max_groups(turn, u):
    v = u + LEAD
    step, group = v // KEYS + 1, v % KEYS
    pair, whose = (turn.pair, CUR) if step < STEPS else (turn.pair.plus(1), NEXT)
    return pair, step % STEPS, group, whose in turn.has


def build(nc, x, w_in, b_qk, b_v, w_out, b_out, gamma, beta, ident_in, out):
    with ExitStack() as ctx:
        def sb(name, shape, dt=F32):
            return ctx.enter_context(nc.sbuf_tensor(name, shape, dt))

        def sem(name):
            return ctx.enter_context(nc.semaphore(name))

        q_stack = sb("q_stack", [P, STEPS, HPS, TOKENS], F32R)
        k_stack = sb("k_stack", [P, STEPS, HPS, TOKENS], F32R)
        parts = sb("parts", [P, 2, 2, TOKENS], F32R)
        x_in = sb("x_in", [P, CT, TOKENS])
        y = sb("y", [P, CT, TOKENS])
        v = sb("v", [P, 2, KEYS, CHANNELS])
        probs = sb("probs", [P, PRING, HPS * TOKENS])
        psum_of_p = sb("psum_of_p", [P, 2, HPS * TOKENS])
        attn = sb("attn", [P, CT, TOKENS])
        o_step = sb("o_step", [P, HALF])
        inv_sum = sb("inv_sum", [P, HALF])
        square = sb("square", [P, CT, HALF])
        rstd = sb("rstd", [P, TOKENS])
        wi = sb("wi", [P, CT, 3 * CHANNELS])
        bqk = sb("bqk", [P, 2 * CT])
        bv = sb("bv", [P, CHANNELS])
        wo = sb("wo", [P, CT, CHANNELS])
        bo = sb("bo", [P, CT])
        gb = sb("gb", [P, 2, CT])
        ident = sb("ident", [P, P])
        ones = sb("ones", [P, DH])
        mean_w = sb("mean_w", [P, P])
        chunk_max = sb("chunk_max", [P, HPS * KEYS, 2])
        row_max = sb("row_max", [P, HPS * KEYS])
        neg_max = sb("neg_max", [P, CROWS, HPS * KEYS], F32R)
        max_rows = sb("max_rows", [CROWS * HPS * KEYS, P], F32R)

        ps_s = ctx.enter_context(nc.psum_tensor("ps_s", [P, HPS, TOKENS], F32))
        ps_m = ctx.enter_context(nc.psum_tensor("ps_m", [P, 2, HALF], F32))
        ps_o = ctx.enter_context(nc.psum_tensor("ps_o", [P, HALF], F32))
        ps_x = ctx.enter_context(nc.psum_tensor("ps_x", [P, HALF], F32))

        const_made = sem("const_made")
        const_loaded = sem("const_loaded")
        x_loaded = sem("x_loaded")
        wo_loaded = sem("wo_loaded")
        res_loaded = sem("res_loaded")
        built = [sem(f"built{s}") for s in range(STEPS)]
        crows_loaded = sem("crows_loaded")
        o_moved = sem("o_moved")
        out_stored = sem("out_stored")
        scores_done = sem("scores_done")
        exp_done = sem("exp_done")
        pv_done = sem("pv_done")
        chunk_done = sem("chunk_done")
        chunk_maxed = sem("chunk_maxed")
        max_split = sem("max_split")
        summed = sem("summed")
        x_filled = sem("x_filled")
        x_freed = sem("x_freed")
        qk_hi = sem("qk_hi")
        o_copied = sem("o_copied")
        o_normed = sem("o_normed")
        sq_done = sem("sq_done")
        rstd_done = sem("rstd_done")
        sqrt_done = sem("sqrt_done")
        y_scaled = sem("y_scaled")
        y_final = sem("y_final")

        N_X, N_WO, N_RES, N_BUILT, N_CROWS, N_OMOVED = 64, 32, 16, 192, 64 * STEPS, 64 * STEPS
        N_S = N_E = 2 * SLOTS
        N_CHUNK = 4 * GROUPS * STEPS
        N_SPLIT, N_SUM = 3 * STEPS, (KEYS - 2) * STEPS

        block = ctx.enter_context(nc.Block())

        @block.sync
        def _(sp):
            def load_x(pair):
                n = pair.number()
                one = bass.ds(n, 1)
                area = bass.ds(n // BATCH, 1)
                sp.dma_start(x_in[:, :, :], x[one].rearrange("a t p n -> p (a t) n")).then_inc(x_loaded, 16)
                sp.dma_start(wi[:, :, :], w_in[area].rearrange("a t p n -> p (a t) n")).then_inc(x_loaded, 16)
                sp.dma_start(bqk[:, :], b_qk[area].rearrange("a p n -> (a p) n")).then_inc(x_loaded, 16)
                sp.dma_start(bv[:, :], b_v[area].partition_broadcast(P).rearrange("p a n -> p (a n)")
                             ).then_inc(x_loaded, 16)

            def build_stack(pair, step):
                for hh in range(HPS):
                    r = DH * ((step * HPS + hh) % 4)
                    for stack, qk, rows in ((q_stack, 0, (0, 0, 1)), (k_stack, 1, (0, 1, 0))):
                        for i, hilo in enumerate(rows):
                            sp.dma_start(stack[DH * i:DH * (i + 1), step, hh, :].bitcast(F32),
                                         parts[r:r + DH, qk, hilo, :].bitcast(F32)).then_inc(built[step], 16)

            def load_crows(turn, pair, step, whose):
                sp.wait_ge(x_freed, turn.filled("maxrow", step) + 1)
                for hh in range(HPS):
                    for part in range(CROWS):
                        r = (part * HPS + hh) * KEYS
                        sp.dma_start(q_stack[QROWS + part:QROWS + part + 1, step, hh, :].bitcast(F32)
                                     .rearrange("o (k n) -> o k n", k=KEYS),
                                     max_rows[r:r + KEYS, :].bitcast(F32)).then_inc(crows_loaded, 16)

            def move_o(turn, pair, step):
                sp.wait_ge(o_normed, pair.at(STEPS, step + 1))
                for hh in range(HPS):
                    r = DH * ((step * HPS + hh) % 4)
                    for lh in range(2):
                        s = DH * (2 * hh + lh)
                        sp.dma_start(attn[r:r + DH, step // 2, lh * HALF:(lh + 1) * HALF],
                                     o_step[s:s + DH, :]).then_inc(o_moved, 16)

            def load_wo(turn, pair):
                area = bass.ds((pair.number() // BATCH), 1)
                if LAST in turn.has:
                    sp.wait_ge(x_freed, turn.filled("outproj", 3) + 1)
                sp.dma_start(wo[:, :, :], w_out[area].rearrange("a t p n -> p (a t) n")).then_inc(wo_loaded, 16)
                sp.dma_start(bo[:, :], b_out[area].rearrange("a p n -> (a p) n")).then_inc(wo_loaded, 16)

            sp.dma_start(ident[:, :], ident_in).then_inc(const_loaded, 16)
            sp.dma_start(gb[:, 0, :], gamma).then_inc(const_loaded, 16)
            sp.dma_start(gb[:, 1, :], beta).then_inc(const_loaded, 16)
            load_x(Pair(None, 0))

            def emit(turn):
                p, nxt, last = turn.pair, turn.pair.plus(1), turn.pair.plus(-1)
                if CUR in turn.has:
                    if LAST in turn.has:
                        sp.wait_ge(scores_done, p.at(N_S, 0))
                    build_stack(p, 3)
                    if NEXT in turn.has:
                        load_x(nxt)
                if LAST in turn.has:
                    move_o(turn, last, 3)
                if CUR in turn.has:
                    load_crows(turn, p, 1, CUR)
                    load_wo(turn, p)
                    move_o(turn, p, 0)
                    load_crows(turn, p, 2, CUR)
                if NEXT in turn.has:
                    sp.wait_ge(x_freed, turn.filled("qk", 3) + 1)
                    for step in range(2):
                        build_stack(nxt, step)
                if LAST in turn.has:
                    n = (last.number())
                    sp.wait_ge(y_final, last.at(2 * CT, 2 * CT))
                    sp.dma_start(out[bass.ds(n, 1)].rearrange("a t p n -> p (a t) n"),
                                 y[:, :, :]).then_inc(out_stored, 16)
                if CUR in turn.has:
                    move_o(turn, p, 1)
                    load_crows(turn, p, 3, CUR)
                    n = (p.number())
                    if LAST in turn.has:
                        sp.wait_ge(out_stored, last.at(16, 16))
                    sp.dma_start(y[:, :, :], x[bass.ds(n, 1)].rearrange("a t p n -> p (a t) n")
                                 ).then_inc(res_loaded, 16)
                    move_o(turn, p, 2)
                if NEXT in turn.has:
                    sp.wait_ge(x_freed, turn.filled("qk", 7) + 1)
                    build_stack(nxt, 2)
                    load_crows(turn, nxt, 0, NEXT)

            turns(sp, emit)
            sp.wait_ge(out_stored, 16 * PAIRS)

        @block.gpsimd
        def _(pool):
            pool.memset(ones[:, :], 1.0).then_inc(const_made, 1)
            pool.memset(mean_w[:, :], 1.0 / CHANNELS).then_inc(const_made, 1)

            def emit(turn):
                if CUR not in turn.has:
                    return
                p = turn.pair
                for s in range(STEPS):
                    acc = psum_of_p[:, s % 2, :]
                    if s >= 2:
                        pool.wait_ge(x_freed, turn.filled("rowsum", s - 2) + 1)
                    elif LAST in turn.has:
                        pool.wait_ge(pv_done, p.at(SLOTS, 0))
                        if s == 1:
                            pool.wait_ge(x_freed, turn.filled("rowsum", 3) + 1)
                        else:
                            pool.wait_ge(x_freed, turn.filled("rowsum", 3))
                    for t in range(1, KEYS - 1):
                        u = s * KEYS + t
                        pool.wait_ge(exp_done, p.at(N_E, 2 * (u + 1)))
                        first = probs[:, (u - 1) % PRING, :] if t == 1 else acc
                        if t > 1:
                            pool.wait_ge(summed, p.at(N_SUM, s * (KEYS - 2) + t - 1))
                        pool.tensor_tensor(acc, first, probs[:, u % PRING, :], ALU.add).then_inc(summed, 1)

            turns(pool, emit)

        @block.scalar
        def _(act):
            def fill_copies(turn, u):
                for slot, kind, i, whose in turn.fill:
                    if slot != u:
                        continue
                    n = turn.filled(kind, i)
                    pair = turn.whose(whose)
                    if kind == "qk":
                        m, half = i // 2, i % 2
                        hi = parts[:, m % 2, 0, half * HALF:(half + 1) * HALF]
                        act.wait_ge(x_filled, n + 1)
                        a, b = (0, 1) if i >= 4 else (2, 3)
                        if i >= 4:
                            act.wait_ge(built[0], pair.at(N_BUILT, N_BUILT))
                            act.wait_ge(built[1], pair.at(N_BUILT, N_BUILT))
                        elif CUR in turn.has:
                            act.wait_ge(built[2], pair.at(N_BUILT, 0))
                            act.wait_ge(built[3], pair.at(N_BUILT, 0))
                        act.activation(hi, ps_x[:, :], ACT.Identity, bias=bqk[:, m:m + 1]).then_inc(qk_hi, 1)
                    elif kind == "maxrow":
                        act.wait_ge(x_filled, n + 1)
                        if not (turn.pair.reg is None and turn.pair.off < 0):
                            before = pair.at(N_CROWS, 64 * i)
                            act.wait_ge(crows_loaded, before)
                        act.activation(max_rows[:, :], ps_x[0:CROWS * HPS * KEYS, 0:P], ACT.Copy
                                       ).then_inc(x_freed, 1)
                    elif kind == "mean":
                        act.wait_ge(x_freed, n + 1)
                        if i == 1:
                            act.wait_ge(x_filled, turn.filled("var", 0) + 1)
                        for m in range(CT):
                            act.activation(square[:, m, :], y[:, m, i * HALF:(i + 1) * HALF],
                                           ACT.Square).then_inc(sq_done, 1)

            def emit(turn):
                p, last = turn.pair, turn.pair.plus(-1)
                for u in range(SLOTS):
                    if CUR in turn.has:
                        for hh in range(HPS):
                            act.wait_ge(scores_done, p.at(N_S, 2 * u + hh + 1))
                            if u >= PRING or LAST in turn.has:
                                b = u - PRING
                                bs, bt = b // KEYS, b % KEYS
                                act.wait_ge(pv_done, p.at(SLOTS, b + 1))
                                if bt == KEYS - 1:
                                    act.wait_ge(x_filled, turn.filled("rowsum", bs % STEPS) + 1)
                                else:
                                    act.wait_ge(summed, p.at(N_SUM, bs * (KEYS - 2) + max(bt, 1)))
                            act.activation(probs[:, u % PRING, hh * TOKENS:(hh + 1) * TOKENS],
                                           ps_s[:, hh, :], ACT.Exp, scale=SCALE).then_inc(exp_done, 1)
                    if u % KEYS == 0 and ((u > 0 and CUR in turn.has) or (u == 0 and LAST in turn.has)):
                        act.wait_ge(pv_done, p.at(SLOTS, u))
                        s = u // KEYS
                        if not (turn.pair.reg is None and turn.pair.off == 0 and s == 1):
                            act.wait_ge(o_moved, p.at(N_OMOVED, 64 * (s - 1)))
                        act.activation(o_step[:, :], ps_o[:, :], ACT.Copy).then_inc(o_copied, 1)
                    if LAST in turn.has and u == 15:
                        act.wait_ge(rstd_done, last.at(2, 2))
                        act.activation(rstd[:, :], rstd[:, :], ACT.Sqrt).then_inc(sqrt_done, 1)
                    if LAST in turn.has and u in (17, 18):
                        half = u - 17
                        for m in range(CT):
                            act.wait_ge(y_scaled, last.at(2 * CT, half * CT + m + 1))
                            t = y[:, m, half * HALF:(half + 1) * HALF]
                            act.activation(t, t, ACT.Identity, bias=gb[:, 1, m:m + 1],
                                           scale=gb[:, 0, m:m + 1]).then_inc(y_final, 1)
                    fill_copies(turn, u)

            act.wait_ge(const_loaded, 48)
            turns(act, emit)

        @block.vector
        def _(dve):
            def fill_copies(turn, u):
                for slot, kind, i, whose in turn.fill:
                    if slot != u:
                        continue
                    n = turn.filled(kind, i)
                    pair = turn.whose(whose)
                    if kind == "rowsum":
                        if not (pair.reg is None and pair.off == 0 and i == 0):
                            dve.wait_ge(o_normed, pair.at(STEPS, i))
                        dve.wait_ge(x_filled, n + 1)
                        for c in range(0, HALF, PIECE):
                            ins = dve.reciprocal(inv_sum[:, c:c + PIECE], ps_x[:, c:c + PIECE])
                        ins.then_inc(x_freed, 1)
                        dve.wait_ge(x_freed, n + 1)
                        dve.wait_ge(o_copied, pair.at(STEPS, i + 1))
                        dve.tensor_tensor(o_step[:, :], o_step[:, :], inv_sum[:, :], ALU.mult
                                          ).then_inc(o_normed, 1)
                    elif kind == "qk":
                        m, half = i // 2, i % 2
                        hi, lo = (parts[:, m % 2, j, half * HALF:(half + 1) * HALF] for j in range(2))
                        dve.wait_ge(qk_hi, pair.at(8, i + 1))
                        dve.scalar_tensor_tensor(out=lo, in0=ps_x[:, :], scalar=bqk[:, m:m + 1],
                                                 in1=hi.bitcast(F32), op0=ALU.add, op1=ALU.subtract
                                                 ).then_inc(x_freed, 1)
                    elif kind == "v":
                        dve.wait_ge(x_filled, n + 1)
                        par = 1 - turn.parity
                        for j in range(2):
                            ins = dve.tensor_tensor(v[:, par, 2 * i + j, :], ps_x[:, j * CHANNELS:(j + 1) * CHANNELS],
                                                    bv[:, :], ALU.add)
                        ins.then_inc(x_freed, 1)
                    elif kind == "outproj":
                        half, m = i // 2, i % 2
                        dve.wait_ge(x_filled, n + 1)
                        dve.wait_ge(res_loaded, pair.at(N_RES, N_RES))
                        t = y[:, m, half * HALF:(half + 1) * HALF]
                        dve.scalar_tensor_tensor(out=t, in0=ps_x[:, :], scalar=bo[:, m:m + 1], in1=t,
                                                 op0=ALU.add, op1=ALU.add).then_inc(x_freed, 1)
                    elif kind == "mean":
                        dve.wait_ge(x_filled, n + 1)
                        for m in range(CT):
                            t = y[:, m, i * HALF:(i + 1) * HALF]
                            ins = dve.tensor_tensor(t, t, ps_x[:, :], ALU.subtract)
                        ins.then_inc(x_freed, 1)
                    elif kind == "var":
                        dve.wait_ge(x_filled, n + 1)
                        t = rstd[:, i * HALF:(i + 1) * HALF]
                        dve.tensor_scalar(t, ps_x[:, :], EPS, None, ALU.add).then_inc(x_freed, 1)
                        dve.wait_ge(x_freed, n + 1)
                        for c in range(0, HALF, PIECE):
                            ins = dve.reciprocal(t[:, c:c + PIECE], t[:, c:c + PIECE])
                        ins.then_inc(rstd_done, 1)

            def emit(turn):
                last = turn.pair.plus(-1)
                for u in range(SLOTS):
                    pair, step, group, exists = max_groups(turn, u)
                    if exists:
                        for i in range(4):
                            c = 4 * group + i
                            col = chunk_max[:, c // 2, c % 2:c % 2 + 1]
                            k = step * 4 * GROUPS + c
                            dve.wait_ge(chunk_done, pair.at(N_CHUNK, k + 1))
                            dve.tensor_reduce(col, ps_m[:, c % 2, :], mybir.AxisListType.X, ALU.max
                                              ).then_inc(chunk_maxed, 1)
                        if group == GROUPS - 1:
                            k = step * 3
                            dve.wait_ge(chunk_maxed, pair.at(N_CHUNK, (step + 1) * 4 * GROUPS))
                            dve.tensor_tensor(row_max[:, :], chunk_max[:, :, 0], chunk_max[:, :, 1],
                                              ALU.max).then_inc(max_split, 1)
                            dve.wait_ge(max_split, pair.at(N_SPLIT, k + 1))
                            if not (pair.reg is None and pair.off == 0 and step == 0):
                                dve.wait_ge(crows_loaded, pair.at(N_CROWS, 64 * step))
                            dve.tensor_scalar(neg_max[:, 0, :], row_max[:, :], -1.0, None, ALU.mult
                                              ).then_inc(max_split, 1)
                            dve.wait_ge(max_split, pair.at(N_SPLIT, k + 2))
                            dve.scalar_tensor_tensor(out=neg_max[:, 1, :], in0=row_max[:, :], scalar=-1.0,
                                                     in1=neg_max[:, 0, :].bitcast(F32), op0=ALU.mult,
                                                     op1=ALU.subtract).then_inc(max_split, 1)
                    fill_copies(turn, u)
                    if LAST in turn.has and u in (16, 17):
                        half = u - 16
                        dve.wait_ge(sqrt_done, last.at(1, 1))
                        for m in range(CT):
                            t = y[:, m, half * HALF:(half + 1) * HALF]
                            dve.tensor_tensor(t, t, rstd[:, half * HALF:(half + 1) * HALF], ALU.mult
                                              ).then_inc(y_scaled, 1)

            dve.memset(k_stack[QROWS:ROWS, :, :, :].bitcast(F32), 1.0).then_inc(const_made, 1)
            turns(dve, emit)

        @block.tensor
        def _(pe):
            pe.wait_ge(const_loaded, 48)
            pe.wait_ge(const_made, 3)

            def scores(turn, u, hh):
                p, s, t = turn.pair, u // KEYS, u % KEYS
                if hh == 0 and t == 0:
                    pe.wait_ge(crows_loaded, p.at(N_CROWS, 64 * (s + 1)))
                if u > 0 or LAST in turn.has:
                    pe.wait_ge(exp_done, p.at(N_E, 2 * (u - 1) + hh + 1))
                for lh in range(2):
                    ins = pe.matmul(ps_s[:, hh, lh * HALF:(lh + 1) * HALF],
                                    k_stack[0:ROWS, s, hh, t * P:(t + 1) * P],
                                    q_stack[0:ROWS, s, hh, lh * HALF:(lh + 1) * HALF], start=True, stop=True)
                ins.then_inc(scores_done, 1)

            def max_chunks(turn, u, which):
                pair, step, group, exists = max_groups(turn, u)
                if not exists:
                    return
                if group == 0 and 0 in which:
                    pe.wait_ge(built[step], pair.at(N_BUILT, N_BUILT))
                for i in which:
                    c = 4 * group + i
                    hh, lt, mh = c // (2 * KEYS), c // 2 % KEYS, c % 2
                    k = step * 4 * GROUPS + c
                    if k >= 2 or not (pair.reg is None and pair.off == 0):
                        pe.wait_ge(chunk_maxed, pair.at(N_CHUNK, k - 1))
                    pe.matmul(ps_m[:, c % 2, :], q_stack[0:QROWS, step, hh, lt * P:(lt + 1) * P],
                              k_stack[0:QROWS, step, hh, mh * HALF:(mh + 1) * HALF],
                              start=True, stop=True).then_inc(chunk_done, 1)

            def weighted(pair, parity, u):
                s, t = u // KEYS, u % KEYS
                pe.wait_ge(exp_done, pair.at(N_E, 2 * (u + 1)))
                if t == 0 and not (pair.reg is None and pair.off == 0 and s == 0):
                    pe.wait_ge(o_copied, pair.at(STEPS, s))
                for hh in range(HPS):
                    h = s * HPS + hh
                    for lh in range(2):
                        j = 2 * hh + lh
                        ins = pe.matmul(ps_o[DH * j:DH * (j + 1), :], v[:, parity, t, h * DH:(h + 1) * DH],
                                        probs[:, u % PRING, j * HALF:(j + 1) * HALF],
                                        start=(t == 0), stop=(t == KEYS - 1), tile_position=(0, DH * j))
                ins.then_inc(pv_done, 1)

            def fill(turn, kind, i, whose):
                n = turn.filled(kind, i)
                pair = turn.whose(whose)
                if not (turn.pair.reg is None and turn.pair.off < 0 and turn.fill[0][1:3] == (kind, i)):
                    pe.wait_ge(x_freed, n)
                if kind == "rowsum":
                    pe.wait_ge(summed, pair.at(N_SUM, (i + 1) * (KEYS - 2)))
                    tail = probs[:, (KEYS * (i + 1) - 1) % PRING, :]
                    for src in (psum_of_p[:, i % 2, :], tail):
                        for j in range(4):
                            ins = pe.matmul(ps_x[DH * j:DH * (j + 1), :], ones[:, :],
                                            src[:, j * HALF:(j + 1) * HALF], start=(src is not tail),
                                            stop=(src is tail), tile_position=(0, DH * j))
                elif kind == "outproj":
                    half, m = i // 2, i % 2
                    pe.wait_ge(o_moved, pair.at(N_OMOVED, N_OMOVED))
                    pe.wait_ge(wo_loaded, pair.at(N_WO, N_WO))
                    for t in range(CT):
                        ins = pe.matmul(ps_x[:, :], wo[:, t, m * P:(m + 1) * P],
                                        attn[:, t, half * HALF:(half + 1) * HALF],
                                        start=(t == 0), stop=(t == CT - 1))
                elif kind == "mean":
                    for t in range(CT):
                        ins = pe.matmul(ps_x[:, :], mean_w[:, :], y[:, t, i * HALF:(i + 1) * HALF],
                                        start=(t == 0), stop=(t == CT - 1))
                elif kind == "var":
                    pe.wait_ge(sq_done, pair.at(2 * CT, (i + 1) * CT))
                    for t in range(CT):
                        ins = pe.matmul(ps_x[:, :], mean_w[:, :], square[:, t, :],
                                        start=(t == 0), stop=(t == CT - 1))
                elif kind == "qk":
                    m, half = i // 2, i % 2
                    col = (m % 2) * CHANNELS + (m // 2) * P
                    pe.wait_ge(x_loaded, pair.at(N_X, N_X))
                    for t in range(CT):
                        ins = pe.matmul(ps_x[:, :], wi[:, t, col:col + P],
                                        x_in[:, t, half * HALF:(half + 1) * HALF],
                                        start=(t == 0), stop=(t == CT - 1))
                elif kind == "v":
                    for j in range(2):
                        kt = 2 * i + j
                        for t in range(CT):
                            ins = pe.matmul(ps_x[:, j * CHANNELS:(j + 1) * CHANNELS],
                                            x_in[:, t, kt * P:(kt + 1) * P], wi[:, t, 2 * CHANNELS:3 * CHANNELS],
                                            start=(t == 0), stop=(t == CT - 1))
                elif kind == "maxrow":
                    pe.wait_ge(max_split, pair.at(N_SPLIT, 3 * (i + 1)))
                    ins = pe.transpose(ps_x[0:CROWS * HPS * KEYS, 0:P],
                                       neg_max[:, :, :].rearrange("p a b -> p (a b)").bitcast(F32), ident[:, :])
                ins.then_inc(x_filled, 1)

            def emit(turn):
                p = turn.pair
                for u in range(SLOTS):
                    if CUR in turn.has:
                        scores(turn, u, 0)
                    max_chunks(turn, u, (0, 1))
                    if u > 0 and CUR in turn.has:
                        weighted(p, turn.parity, u - 1)
                    elif u == 0 and LAST in turn.has:
                        weighted(p.plus(-1), 1 - turn.parity, SLOTS - 1)
                    if CUR in turn.has:
                        scores(turn, u, 1)
                    max_chunks(turn, u, (2, 3))
                    for slot, kind, i, whose in turn.fill:
                        if slot == u:
                            fill(turn, kind, i, whose)

            turns(pe, emit)


_ORDER = ("x", "w_in", "b_qk", "b_v", "w_out", "b_out", "gamma", "beta", "ident")


def kernel(x, L0_conv_W_in, L0_conv_b_in, L0_conv_W_out, L0_conv_b_out, L0_conv_gamma, L0_conv_beta):
    import numpy as np
    import concourse.bacc as bacc
    from concourse.bass_utils import run_bass_kernel_spmd

    rows, cols = HEIGHT // SPLIT, WIDTH // SPLIT
    a = {}
    t = np.asarray(x).reshape(BATCH, CHANNELS, SPLIT, rows, SPLIT, cols).transpose(2, 4, 0, 1, 3, 5)
    a["x"] = t.reshape(PAIRS, CT, P, TOKENS)
    a["w_in"] = np.asarray(L0_conv_W_in).transpose(0, 2, 1).reshape(AREAS, CT, P, 3 * CHANNELS)
    b_in = np.asarray(L0_conv_b_in)
    a["b_qk"] = b_in[:, :2 * CHANNELS].reshape(AREAS, 2, CT, P).transpose(0, 3, 2, 1).reshape(AREAS, P, 2 * CT)
    a["b_v"] = b_in[:, 2 * CHANNELS:]
    a["w_out"] = np.asarray(L0_conv_W_out).transpose(0, 2, 1).reshape(AREAS, CT, P, CHANNELS)
    a["b_out"] = np.asarray(L0_conv_b_out).reshape(AREAS, CT, P).transpose(0, 2, 1)
    a["gamma"] = np.asarray(L0_conv_gamma).reshape(CT, P).T
    a["beta"] = np.asarray(L0_conv_beta).reshape(CT, P).T
    a["ident"] = np.eye(P, dtype=np.float32)
    a = {k: np.ascontiguousarray(v) for k, v in a.items()}

    nc = bacc.Bacc("TRN2", target_bir_lowering=False, num_devices=1)
    ins = [nc.dram_tensor(f"in_{k}", a[k].shape, F32, kind="ExternalInput").ap() for k in _ORDER]
    out = nc.dram_tensor("out_y", (PAIRS, CT, P, TOKENS), F32, kind="ExternalOutput").ap()
    build(nc, *ins, out)
    r = run_bass_kernel_spmd(nc, [{f"in_{k}": a[k] for k in _ORDER}], core_ids=[0])
    got = np.asarray(r.results[0]["out_y"]).reshape(SPLIT, SPLIT, BATCH, CHANNELS, rows, cols)
    return np.ascontiguousarray(got.transpose(2, 3, 0, 4, 1, 5)).reshape(BATCH, CHANNELS, HEIGHT, WIDTH)
```

```python
from contextlib import ExitStack

import concourse.bass as bass
from concourse import mybir

F32 = mybir.dt.float32
F32R = mybir.dt.float32r
ALU = mybir.AluOpType
ACT = mybir.ActivationFunctionType

BATCH, CHANNELS, HEIGHT, WIDTH = 8, 256, 64, 64
SPLIT = 2
AREAS = SPLIT * SPLIT
HEADS = 8
DH = CHANNELS // HEADS
TOKENS = HEIGHT * WIDTH // AREAS
PAIRS = AREAS * BATCH
EPS = 1e-5
SCALE = float(DH) ** -0.5

P = 128
CT = CHANNELS // P
HALF = TOKENS // 2
HPS = 2
STEPS = HEADS // HPS
KEYS = TOKENS // P
SLOTS = STEPS * KEYS
LEAD = 2
GROUPS = 8
PRING = 4
QROWS = 3 * DH
CROWS = 2
ROWS = QROWS + CROWS
PIECE = 128


class Pair:

    def __init__(self, reg, off):
        self.reg, self.off = reg, off

    def at(self, n, k):
        return self.off * n + k if self.reg is None else self.reg * (2 * n) + (self.off * n + k)

    def plus(self, k):
        return Pair(self.reg, self.off + k)

    def number(self):
        return self.off if self.reg is None else self.reg * 2 + self.off


LAST, CUR, NEXT = "last", "cur", "next"
FILL = [
    (2, "rowsum", 3, LAST),
    (5, "outproj", 0, LAST), (6, "maxrow", 1, CUR), (6, "outproj", 1, LAST),
    (7, "outproj", 2, LAST), (8, "outproj", 3, LAST),
    (9, "mean", 0, LAST), (10, "rowsum", 0, CUR), (11, "mean", 1, LAST),
    (12, "var", 0, LAST), (13, "var", 1, LAST),
    (14, "maxrow", 2, CUR), (14, "qk", 0, NEXT), (15, "qk", 1, NEXT), (16, "qk", 2, NEXT),
    (17, "qk", 3, NEXT), (18, "rowsum", 1, CUR),
    (19, "v", 0, NEXT), (20, "v", 1, NEXT), (21, "v", 2, NEXT),
    (22, "maxrow", 3, CUR), (22, "v", 3, NEXT),
    (23, "qk", 4, NEXT), (24, "qk", 5, NEXT), (25, "qk", 6, NEXT), (26, "rowsum", 2, CUR),
    (27, "qk", 7, NEXT), (30, "maxrow", 0, NEXT),
]


def fills(has):
    return [f for f in FILL if f[3] in has]


class Turn:

    def __init__(self, pair, parity, has):
        self.pair, self.parity, self.has = pair, parity, has
        self.fill = fills(has)

    def filled(self, kind, index):
        n = [(k, i) for _, k, i, _ in self.fill].index((kind, index))
        first = len(fills((NEXT,)))
        second = first + len(fills((CUR, NEXT)))
        full = len(FILL)
        if self.pair.reg is None:
            p = self.pair.off
            if p < 0:
                return n
            if p == 0:
                return first + n
            if p == PAIRS:
                return second + (PAIRS - 2) * full + len(fills((LAST, CUR))) + n
        return self.pair.at(full, second - full + n)

    def whose(self, name):
        return self.pair.plus({LAST: -1, CUR: 0, NEXT: 1}[name])


def turns(engine, emit):
    emit(Turn(Pair(None, -1), 1, (NEXT,)))
    emit(Turn(Pair(None, 0), 0, (CUR, NEXT)))
    with engine.Fori(0, PAIRS // 2 - 1) as i:
        emit(Turn(Pair(i, 1), 1, (LAST, CUR, NEXT)))
        emit(Turn(Pair(i, 2), 0, (LAST, CUR, NEXT)))
    emit(Turn(Pair(None, PAIRS - 1), 1, (LAST, CUR)))
    emit(Turn(Pair(None, PAIRS), 0, (LAST,)))


def max_groups(turn, u):
    v = u + LEAD
    step, group = v // KEYS + 1, v % KEYS
    pair, whose = (turn.pair, CUR) if step < STEPS else (turn.pair.plus(1), NEXT)
    return pair, step % STEPS, group, whose in turn.has


def build(nc, x, w_in, b_qk, b_v, w_out, b_out, gamma, beta, ident_in, out):
    with ExitStack() as ctx:
        def sb(name, shape, dt=F32):
            return ctx.enter_context(nc.sbuf_tensor(name, shape, dt))

        def sem(name):
            return ctx.enter_context(nc.semaphore(name))

        q_stack = sb("q_stack", [P, STEPS, HPS, TOKENS], F32R)
        k_stack = sb("k_stack", [P, STEPS, HPS, TOKENS], F32R)
        parts = sb("parts", [P, 2, 2, TOKENS], F32R)
        x_in = sb("x_in", [P, CT, TOKENS])
        y = sb("y", [P, CT, TOKENS])
        v = sb("v", [P, 2, KEYS, CHANNELS])
        probs = sb("probs", [P, PRING, HPS * TOKENS])
        psum_of_p = sb("psum_of_p", [P, 2, HPS * TOKENS])
        attn = sb("attn", [P, CT, TOKENS])
        o_step = sb("o_step", [P, HALF])
        inv_sum = sb("inv_sum", [P, HALF])
        square = sb("square", [P, CT, HALF])
        rstd = sb("rstd", [P, TOKENS])
        stat_t = sb("stat_t", [P, HALF])
        inv_col = sb("inv_col", [P, HALF // 32])
        var_col = sb("var_col", [P, 2, HALF // 32])
        rstd_col = sb("rstd_col", [P, 2, HALF // 32])
        wi = sb("wi", [P, CT, 3 * CHANNELS])
        bqk = sb("bqk", [P, 2 * CT])
        bv = sb("bv", [P, CHANNELS])
        wo = sb("wo", [P, CT, CHANNELS])
        bo = sb("bo", [P, CT])
        gb = sb("gb", [P, 2, CT])
        ident = sb("ident", [P, P])
        ones = sb("ones", [P, DH])
        mean_w = sb("mean_w", [P, P])
        chunk_max = sb("chunk_max", [P, HPS * KEYS, 2])
        row_max = sb("row_max", [P, HPS * KEYS])
        neg_max = sb("neg_max", [P, CROWS, HPS * KEYS], F32R)
        max_rows = sb("max_rows", [CROWS * HPS * KEYS, P], F32R)

        ps_s = ctx.enter_context(nc.psum_tensor("ps_s", [P, HPS, TOKENS], F32))
        ps_m = ctx.enter_context(nc.psum_tensor("ps_m", [P, 2, HALF], F32))
        ps_o = ctx.enter_context(nc.psum_tensor("ps_o", [P, HALF], F32))
        ps_x = ctx.enter_context(nc.psum_tensor("ps_x", [P, HALF], F32))

        const_made = sem("const_made")
        const_loaded = sem("const_loaded")
        x_loaded = sem("x_loaded")
        wo_loaded = sem("wo_loaded")
        res_loaded = sem("res_loaded")
        built = [sem(f"built{s}") for s in range(STEPS)]
        crows_loaded = sem("crows_loaded")
        o_moved = sem("o_moved")
        out_stored = sem("out_stored")
        scores_done = sem("scores_done")
        exp_done = sem("exp_done")
        pv_done = sem("pv_done")
        chunk_done = sem("chunk_done")
        chunk_maxed = sem("chunk_maxed")
        max_split = sem("max_split")
        summed = sem("summed")
        x_filled = sem("x_filled")
        x_freed = sem("x_freed")
        qk_hi = sem("qk_hi")
        o_copied = sem("o_copied")
        o_normed = sem("o_normed")
        sq_done = sem("sq_done")
        inv_made = sem("inv_made")
        inv_spread = sem("inv_spread")
        var_read = sem("var_read")
        rstd_done = sem("rstd_done")
        rstd_spread = sem("rstd_spread")
        sqrt_done = sem("sqrt_done")
        y_scaled = sem("y_scaled")
        y_final = sem("y_final")

        N_X, N_WO, N_RES, N_BUILT, N_CROWS, N_OMOVED = 64, 32, 16, 192, 64 * STEPS, 64 * STEPS
        N_S = N_E = 2 * SLOTS
        N_CHUNK = 4 * GROUPS * STEPS
        N_SPLIT, N_SUM = 3 * STEPS, (KEYS - 2) * STEPS

        block = ctx.enter_context(nc.Block())

        @block.sync
        def _(sp):
            def load_x(pair):
                n = pair.number()
                one = bass.ds(n, 1)
                area = bass.ds(n // BATCH, 1)
                sp.dma_start(x_in[:, :, :], x[one].rearrange("a t p n -> p (a t) n")).then_inc(x_loaded, 16)
                sp.dma_start(wi[:, :, :], w_in[area].rearrange("a t p n -> p (a t) n")).then_inc(x_loaded, 16)
                sp.dma_start(bqk[:, :], b_qk[area].rearrange("a p n -> (a p) n")).then_inc(x_loaded, 16)
                sp.dma_start(bv[:, :], b_v[area].partition_broadcast(P).rearrange("p a n -> p (a n)")
                             ).then_inc(x_loaded, 16)

            def build_stack(pair, step):
                for hh in range(HPS):
                    r = DH * ((step * HPS + hh) % 4)
                    for stack, qk, rows in ((q_stack, 0, (0, 0, 1)), (k_stack, 1, (0, 1, 0))):
                        for i, hilo in enumerate(rows):
                            sp.dma_start(stack[DH * i:DH * (i + 1), step, hh, :].bitcast(F32),
                                         parts[r:r + DH, qk, hilo, :].bitcast(F32)).then_inc(built[step], 16)

            def load_crows(turn, pair, step, whose):
                sp.wait_ge(x_freed, turn.filled("maxrow", step) + 1)
                for hh in range(HPS):
                    for part in range(CROWS):
                        r = (part * HPS + hh) * KEYS
                        sp.dma_start(q_stack[QROWS + part:QROWS + part + 1, step, hh, :].bitcast(F32)
                                     .rearrange("o (k n) -> o k n", k=KEYS),
                                     max_rows[r:r + KEYS, :].bitcast(F32)).then_inc(crows_loaded, 16)

            def move_o(turn, pair, step):
                sp.wait_ge(o_normed, pair.at(STEPS, step + 1))
                for hh in range(HPS):
                    r = DH * ((step * HPS + hh) % 4)
                    for lh in range(2):
                        s = DH * (2 * hh + lh)
                        sp.dma_start(attn[r:r + DH, step // 2, lh * HALF:(lh + 1) * HALF],
                                     o_step[s:s + DH, :]).then_inc(o_moved, 16)

            def load_wo(turn, pair):
                area = bass.ds((pair.number() // BATCH), 1)
                if LAST in turn.has:
                    sp.wait_ge(x_freed, turn.filled("outproj", 3) + 1)
                sp.dma_start(wo[:, :, :], w_out[area].rearrange("a t p n -> p (a t) n")).then_inc(wo_loaded, 16)
                sp.dma_start(bo[:, :], b_out[area].rearrange("a p n -> (a p) n")).then_inc(wo_loaded, 16)

            sp.dma_start(ident[:, :], ident_in).then_inc(const_loaded, 16)
            sp.dma_start(gb[:, 0, :], gamma).then_inc(const_loaded, 16)
            sp.dma_start(gb[:, 1, :], beta).then_inc(const_loaded, 16)
            load_x(Pair(None, 0))

            def emit(turn):
                p, nxt, last = turn.pair, turn.pair.plus(1), turn.pair.plus(-1)
                if CUR in turn.has:
                    if LAST in turn.has:
                        sp.wait_ge(scores_done, p.at(N_S, 0))
                    build_stack(p, 3)
                    if NEXT in turn.has:
                        load_x(nxt)
                if LAST in turn.has:
                    move_o(turn, last, 3)
                if CUR in turn.has:
                    load_crows(turn, p, 1, CUR)
                    load_wo(turn, p)
                    move_o(turn, p, 0)
                    load_crows(turn, p, 2, CUR)
                if NEXT in turn.has:
                    sp.wait_ge(x_freed, turn.filled("qk", 3) + 1)
                    for step in range(2):
                        build_stack(nxt, step)
                if LAST in turn.has:
                    n = (last.number())
                    sp.wait_ge(y_final, last.at(2 * CT, 2 * CT))
                    sp.dma_start(out[bass.ds(n, 1)].rearrange("a t p n -> p (a t) n"),
                                 y[:, :, :]).then_inc(out_stored, 16)
                if CUR in turn.has:
                    move_o(turn, p, 1)
                    load_crows(turn, p, 3, CUR)
                    n = (p.number())
                    if LAST in turn.has:
                        sp.wait_ge(out_stored, last.at(16, 16))
                    sp.dma_start(y[:, :, :], x[bass.ds(n, 1)].rearrange("a t p n -> p (a t) n")
                                 ).then_inc(res_loaded, 16)
                    move_o(turn, p, 2)
                if NEXT in turn.has:
                    sp.wait_ge(x_freed, turn.filled("qk", 7) + 1)
                    build_stack(nxt, 2)
                    load_crows(turn, nxt, 0, NEXT)

            turns(sp, emit)
            sp.wait_ge(out_stored, 16 * PAIRS)

        @block.gpsimd
        def _(pool):
            pool.memset(ones[:, :], 1.0).then_inc(const_made, 1)
            pool.memset(mean_w[:, :], 1.0 / CHANNELS).then_inc(const_made, 1)

            def emit(turn):
                if CUR not in turn.has:
                    return
                p = turn.pair
                for s in range(STEPS):
                    acc = psum_of_p[:, s % 2, :]
                    if s >= 2:
                        pool.wait_ge(x_freed, turn.filled("rowsum", s - 2) + 1)
                    elif LAST in turn.has:
                        pool.wait_ge(pv_done, p.at(SLOTS, 0))
                        if s == 1:
                            pool.wait_ge(x_freed, turn.filled("rowsum", 3) + 1)
                        else:
                            pool.wait_ge(x_freed, turn.filled("rowsum", 3))
                    for t in range(1, KEYS - 1):
                        u = s * KEYS + t
                        pool.wait_ge(exp_done, p.at(N_E, 2 * (u + 1)))
                        first = probs[:, (u - 1) % PRING, :] if t == 1 else acc
                        if t > 1:
                            pool.wait_ge(summed, p.at(N_SUM, s * (KEYS - 2) + t - 1))
                        pool.tensor_tensor(acc, first, probs[:, u % PRING, :], ALU.add).then_inc(summed, 1)

            turns(pool, emit)

        @block.scalar
        def _(act):
            def fill_copies(turn, u):
                for slot, kind, i, whose in turn.fill:
                    if slot + (kind == "mean") != u:
                        continue
                    n = turn.filled(kind, i)
                    pair = turn.whose(whose)
                    if kind == "qk":
                        m, half = i // 2, i % 2
                        hi = parts[:, m % 2, 0, half * HALF:(half + 1) * HALF]
                        act.wait_ge(x_filled, n + 1)
                        a, b = (0, 1) if i >= 4 else (2, 3)
                        if i >= 4:
                            act.wait_ge(built[0], pair.at(N_BUILT, N_BUILT))
                            act.wait_ge(built[1], pair.at(N_BUILT, N_BUILT))
                        elif CUR in turn.has:
                            act.wait_ge(built[2], pair.at(N_BUILT, 0))
                            act.wait_ge(built[3], pair.at(N_BUILT, 0))
                        act.activation(hi, ps_x[:, :], ACT.Identity, bias=bqk[:, m:m + 1]).then_inc(qk_hi, 1)
                    elif kind == "maxrow":
                        act.wait_ge(x_filled, n + 1)
                        if not (turn.pair.reg is None and turn.pair.off < 0):
                            before = pair.at(N_CROWS, 64 * i)
                            act.wait_ge(crows_loaded, before)
                        act.activation(max_rows[:, :], ps_x[0:CROWS * HPS * KEYS, 0:P], ACT.Copy
                                       ).then_inc(x_freed, 1)
                    elif kind == "mean":
                        act.wait_ge(x_freed, n + 1)
                        if i == 1:
                            act.wait_ge(x_filled, turn.filled("var", 0) + 1)
                        for m in range(CT):
                            act.activation(square[:, m, :], y[:, m, i * HALF:(i + 1) * HALF],
                                           ACT.Square).then_inc(sq_done, 1)

            def emit(turn):
                p, last = turn.pair, turn.pair.plus(-1)
                for u in range(SLOTS):
                    if CUR in turn.has:
                        for hh in range(HPS):
                            act.wait_ge(scores_done, p.at(N_S, 2 * u + hh + 1))
                            if u >= PRING or LAST in turn.has:
                                b = u - PRING
                                bs, bt = b // KEYS, b % KEYS
                                act.wait_ge(pv_done, p.at(SLOTS, b + 1))
                                if bt == KEYS - 1:
                                    act.wait_ge(x_filled, turn.filled("rowsum", bs % STEPS) + 1)
                                else:
                                    act.wait_ge(summed, p.at(N_SUM, bs * (KEYS - 2) + max(bt, 1)))
                            act.activation(probs[:, u % PRING, hh * TOKENS:(hh + 1) * TOKENS],
                                           ps_s[:, hh, :], ACT.Exp, scale=SCALE).then_inc(exp_done, 1)
                    if u % KEYS == 0 and ((u > 0 and CUR in turn.has) or (u == 0 and LAST in turn.has)):
                        act.wait_ge(pv_done, p.at(SLOTS, u))
                        s = u // KEYS
                        if not (turn.pair.reg is None and turn.pair.off == 0 and s == 1):
                            act.wait_ge(o_moved, p.at(N_OMOVED, 64 * (s - 1)))
                        act.activation(o_step[:, :], ps_o[:, :], ACT.Copy).then_inc(o_copied, 1)
                    if LAST in turn.has and u == 15:
                        act.wait_ge(rstd_done, last.at(2, 2))
                        act.activation(rstd_col[:, :, :], rstd_col[:, :, :], ACT.Sqrt).then_inc(sqrt_done, 1)
                    if LAST in turn.has and u in (17, 18):
                        half = u - 17
                        for m in range(CT):
                            act.wait_ge(y_scaled, last.at(2 * CT, half * CT + m + 1))
                            t = y[:, m, half * HALF:(half + 1) * HALF]
                            act.activation(t, t, ACT.Identity, bias=gb[:, 1, m:m + 1],
                                           scale=gb[:, 0, m:m + 1]).then_inc(y_final, 1)
                    fill_copies(turn, u)

            act.wait_ge(const_loaded, 48)
            turns(act, emit)

        @block.vector
        def _(dve):
            def spread(col):
                return col.unsqueeze(2).broadcast_to([P, HALF // 32, 32])

            def after_fill(turn, u, place):
                for slot, kind, i, whose in turn.fill:
                    if slot != u:
                        continue
                    n = turn.filled(kind, i)
                    pair = turn.whose(whose)
                    if kind == "rowsum":
                        if place == 0:
                            dve.wait_ge(x_filled, n + 1)
                            dve.transpose(stat_t[:, :], ps_x[:, :]).then_inc(x_freed, 1)
                        elif place == 1:
                            dve.wait_ge(x_freed, n + 1)
                            dve.reciprocal(inv_col[:, :], stat_t[:, 0:HALF:32]).then_inc(inv_made, 1)
                        elif place == 2:
                            dve.wait_ge(inv_made, pair.at(STEPS, i + 1))
                            dve.transpose(inv_sum[:, :], spread(inv_col[:, :])).then_inc(inv_spread, 1)
                        elif place == 3:
                            dve.wait_ge(inv_spread, pair.at(STEPS, i + 1))
                            dve.wait_ge(o_copied, pair.at(STEPS, i + 1))
                            dve.tensor_tensor(o_step[:, :], o_step[:, :], inv_sum[:, :], ALU.mult
                                              ).then_inc(o_normed, 1)
                    elif kind == "qk" and place == 1:
                        m, half = i // 2, i % 2
                        hi, lo = (parts[:, m % 2, j, half * HALF:(half + 1) * HALF] for j in range(2))
                        dve.wait_ge(qk_hi, pair.at(8, i + 1))
                        dve.scalar_tensor_tensor(out=lo, in0=ps_x[:, :], scalar=bqk[:, m:m + 1],
                                                 in1=hi.bitcast(F32), op0=ALU.add, op1=ALU.subtract
                                                 ).then_inc(x_freed, 1)
                    elif kind == "v" and place == 0:
                        dve.wait_ge(x_filled, n + 1)
                        par = 1 - turn.parity
                        for j in range(2):
                            ins = dve.tensor_tensor(v[:, par, 2 * i + j, :], ps_x[:, j * CHANNELS:(j + 1) * CHANNELS],
                                                    bv[:, :], ALU.add)
                        ins.then_inc(x_freed, 1)
                    elif kind == "outproj" and place == 0:
                        half, m = i // 2, i % 2
                        dve.wait_ge(x_filled, n + 1)
                        dve.wait_ge(res_loaded, pair.at(N_RES, N_RES))
                        t = y[:, m, half * HALF:(half + 1) * HALF]
                        dve.scalar_tensor_tensor(out=t, in0=ps_x[:, :], scalar=bo[:, m:m + 1], in1=t,
                                                 op0=ALU.add, op1=ALU.add).then_inc(x_freed, 1)
                    elif kind == "mean" and place == 0:
                        dve.wait_ge(x_filled, n + 1)
                        for m in range(CT):
                            t = y[:, m, i * HALF:(i + 1) * HALF]
                            ins = dve.tensor_tensor(t, t, ps_x[:, :], ALU.subtract)
                        ins.then_inc(x_freed, 1)
                    elif kind == "var":
                        if place == 0:
                            dve.wait_ge(x_filled, n + 1)
                            dve.transpose(stat_t[:, :], ps_x[:, :]).then_inc(x_freed, 1)
                        elif place == 1:
                            dve.wait_ge(x_freed, n + 1)
                            dve.tensor_scalar(var_col[:, i, :], stat_t[:, 0:HALF:32], EPS, None, ALU.add
                                              ).then_inc(var_read, 1)
                        elif place == 2:
                            dve.wait_ge(var_read, pair.at(2, i + 1))
                            dve.reciprocal(rstd_col[:, i, :], var_col[:, i, :]).then_inc(rstd_done, 1)

            def emit(turn):
                last = turn.pair.plus(-1)
                for u in range(SLOTS):
                    pair, step, group, exists = max_groups(turn, u)
                    for i in range(4):
                        after_fill(turn, u - 1, i)
                        if LAST in turn.has and u == 15 and i >= 2:
                            dve.wait_ge(sqrt_done, last.at(1, 1))
                            half = i - 2
                            dve.transpose(rstd[:, half * HALF:(half + 1) * HALF], spread(rstd_col[:, half, :])
                                          ).then_inc(rstd_spread, 1)
                        if LAST in turn.has and u in (16, 17) and i in (1, 3):
                            m, half = i // 2, u - 16
                            dve.wait_ge(rstd_spread, last.at(2, 2))
                            t = y[:, m, half * HALF:(half + 1) * HALF]
                            dve.tensor_tensor(t, t, rstd[:, half * HALF:(half + 1) * HALF], ALU.mult
                                              ).then_inc(y_scaled, 1)
                        if exists:
                            c = 4 * group + i
                            col = chunk_max[:, c // 2, c % 2:c % 2 + 1]
                            k = step * 4 * GROUPS + c
                            dve.wait_ge(chunk_done, pair.at(N_CHUNK, k + 1))
                            dve.tensor_reduce(col, ps_m[:, c % 2, :], mybir.AxisListType.X, ALU.max
                                              ).then_inc(chunk_maxed, 1)
                    if exists:
                        if group == GROUPS - 1:
                            k = step * 3
                            dve.wait_ge(chunk_maxed, pair.at(N_CHUNK, (step + 1) * 4 * GROUPS))
                            dve.tensor_tensor(row_max[:, :], chunk_max[:, :, 0], chunk_max[:, :, 1],
                                              ALU.max).then_inc(max_split, 1)
                            dve.wait_ge(max_split, pair.at(N_SPLIT, k + 1))
                            if not (pair.reg is None and pair.off == 0 and step == 0):
                                dve.wait_ge(crows_loaded, pair.at(N_CROWS, 64 * step))
                            dve.tensor_scalar(neg_max[:, 0, :], row_max[:, :], -1.0, None, ALU.mult
                                              ).then_inc(max_split, 1)
                            dve.wait_ge(max_split, pair.at(N_SPLIT, k + 2))
                            dve.scalar_tensor_tensor(out=neg_max[:, 1, :], in0=row_max[:, :], scalar=-1.0,
                                                     in1=neg_max[:, 0, :].bitcast(F32), op0=ALU.mult,
                                                     op1=ALU.subtract).then_inc(max_split, 1)

            dve.memset(k_stack[QROWS:ROWS, :, :, :].bitcast(F32), 1.0).then_inc(const_made, 1)
            turns(dve, emit)

        @block.tensor
        def _(pe):
            pe.wait_ge(const_loaded, 48)
            pe.wait_ge(const_made, 3)

            def scores(turn, u, hh):
                p, s, t = turn.pair, u // KEYS, u % KEYS
                if hh == 0 and t == 0:
                    pe.wait_ge(crows_loaded, p.at(N_CROWS, 64 * (s + 1)))
                if u > 0 or LAST in turn.has:
                    pe.wait_ge(exp_done, p.at(N_E, 2 * (u - 1) + hh + 1))
                for lh in range(2):
                    ins = pe.matmul(ps_s[:, hh, lh * HALF:(lh + 1) * HALF],
                                    k_stack[0:ROWS, s, hh, t * P:(t + 1) * P],
                                    q_stack[0:ROWS, s, hh, lh * HALF:(lh + 1) * HALF], start=True, stop=True)
                ins.then_inc(scores_done, 1)

            def max_chunks(turn, u, which):
                pair, step, group, exists = max_groups(turn, u)
                if not exists:
                    return
                if group == 0 and 0 in which:
                    pe.wait_ge(built[step], pair.at(N_BUILT, N_BUILT))
                for i in which:
                    c = 4 * group + i
                    hh, lt, mh = c // (2 * KEYS), c // 2 % KEYS, c % 2
                    k = step * 4 * GROUPS + c
                    if k >= 2 or not (pair.reg is None and pair.off == 0):
                        pe.wait_ge(chunk_maxed, pair.at(N_CHUNK, k - 1))
                    pe.matmul(ps_m[:, c % 2, :], q_stack[0:QROWS, step, hh, lt * P:(lt + 1) * P],
                              k_stack[0:QROWS, step, hh, mh * HALF:(mh + 1) * HALF],
                              start=True, stop=True).then_inc(chunk_done, 1)

            def weighted(pair, parity, u):
                s, t = u // KEYS, u % KEYS
                pe.wait_ge(exp_done, pair.at(N_E, 2 * (u + 1)))
                if t == 0 and not (pair.reg is None and pair.off == 0 and s == 0):
                    pe.wait_ge(o_copied, pair.at(STEPS, s))
                for hh in range(HPS):
                    h = s * HPS + hh
                    for lh in range(2):
                        j = 2 * hh + lh
                        ins = pe.matmul(ps_o[DH * j:DH * (j + 1), :], v[:, parity, t, h * DH:(h + 1) * DH],
                                        probs[:, u % PRING, j * HALF:(j + 1) * HALF],
                                        start=(t == 0), stop=(t == KEYS - 1), tile_position=(0, DH * j))
                ins.then_inc(pv_done, 1)

            def fill(turn, kind, i, whose, part):
                n = turn.filled(kind, i)
                pair = turn.whose(whose)
                if part == 0 and not (turn.pair.reg is None and turn.pair.off < 0 and n == 0):
                    pe.wait_ge(x_freed, n)
                first, last = part == 0, part == 1
                if kind == "rowsum":
                    if part == 0:
                        src = probs[:, (KEYS * (i + 1) - 1) % PRING, :]
                    else:
                        pe.wait_ge(summed, pair.at(N_SUM, (i + 1) * (KEYS - 2)))
                        src = psum_of_p[:, i % 2, :]
                    for j in range(4):
                        ins = pe.matmul(ps_x[DH * j:DH * (j + 1), :], ones[:, :], src[:, j * HALF:(j + 1) * HALF],
                                        start=first, stop=last, tile_position=(0, DH * j))
                elif kind == "outproj":
                    half, m = i // 2, i % 2
                    if part == 0:
                        pe.wait_ge(o_moved, pair.at(N_OMOVED, N_OMOVED))
                        pe.wait_ge(wo_loaded, pair.at(N_WO, N_WO))
                    ins = pe.matmul(ps_x[:, :], wo[:, part, m * P:(m + 1) * P],
                                    attn[:, part, half * HALF:(half + 1) * HALF], start=first, stop=last)
                elif kind == "mean":
                    ins = pe.matmul(ps_x[:, :], mean_w[:, :], y[:, part, i * HALF:(i + 1) * HALF],
                                    start=first, stop=last)
                elif kind == "var":
                    pe.wait_ge(sq_done, pair.at(2 * CT, i * CT + part + 1))
                    ins = pe.matmul(ps_x[:, :], mean_w[:, :], square[:, part, :], start=first, stop=last)
                elif kind == "qk":
                    m, half = i // 2, i % 2
                    col = (m % 2) * CHANNELS + (m // 2) * P
                    pe.wait_ge(x_loaded, pair.at(N_X, N_X))
                    ins = pe.matmul(ps_x[:, :], wi[:, part, col:col + P],
                                    x_in[:, part, half * HALF:(half + 1) * HALF], start=first, stop=last)
                elif kind == "v":
                    kt = 2 * i + part
                    for t in range(CT):
                        ins = pe.matmul(ps_x[:, part * CHANNELS:(part + 1) * CHANNELS],
                                        x_in[:, t, kt * P:(kt + 1) * P], wi[:, t, 2 * CHANNELS:3 * CHANNELS],
                                        start=(t == 0), stop=(t == CT - 1))
                elif kind == "maxrow":
                    pe.wait_ge(max_split, pair.at(N_SPLIT, 3 * (i + 1)))
                    ins = pe.transpose(ps_x[0:CROWS * HPS * KEYS, 0:P],
                                       neg_max[:, :, :].rearrange("p a b -> p (a b)").bitcast(F32), ident[:, :])
                if last or kind == "maxrow":
                    ins.then_inc(x_filled, 1)

            def emit(turn):
                p = turn.pair
                for u in range(SLOTS):
                    if CUR in turn.has:
                        scores(turn, u, 0)
                    max_chunks(turn, u, (0,))
                    if u > 0 and CUR in turn.has:
                        weighted(p, turn.parity, u - 1)
                    elif u == 0 and LAST in turn.has:
                        weighted(p.plus(-1), 1 - turn.parity, SLOTS - 1)
                    max_chunks(turn, u, (1,))
                    for slot, kind, i, whose in turn.fill:
                        if slot == u and kind == "maxrow":
                            fill(turn, kind, i, whose, 0)
                    if CUR in turn.has:
                        scores(turn, u, 1)
                    max_chunks(turn, u, (2,))
                    for part in range(2):
                        for slot, kind, i, whose in turn.fill:
                            if slot == u and kind != "maxrow":
                                fill(turn, kind, i, whose, part)
                        if part == 0:
                            max_chunks(turn, u, (3,))

            turns(pe, emit)


_ORDER = ("x", "w_in", "b_qk", "b_v", "w_out", "b_out", "gamma", "beta", "ident")


def kernel(x, L0_conv_W_in, L0_conv_b_in, L0_conv_W_out, L0_conv_b_out, L0_conv_gamma, L0_conv_beta):
    import numpy as np
    import concourse.bacc as bacc
    from concourse.bass_utils import run_bass_kernel_spmd

    rows, cols = HEIGHT // SPLIT, WIDTH // SPLIT
    a = {}
    t = np.asarray(x).reshape(BATCH, CHANNELS, SPLIT, rows, SPLIT, cols).transpose(2, 4, 0, 1, 3, 5)
    a["x"] = t.reshape(PAIRS, CT, P, TOKENS)
    a["w_in"] = np.asarray(L0_conv_W_in).transpose(0, 2, 1).reshape(AREAS, CT, P, 3 * CHANNELS)
    b_in = np.asarray(L0_conv_b_in)
    a["b_qk"] = b_in[:, :2 * CHANNELS].reshape(AREAS, 2, CT, P).transpose(0, 3, 2, 1).reshape(AREAS, P, 2 * CT)
    a["b_v"] = b_in[:, 2 * CHANNELS:]
    a["w_out"] = np.asarray(L0_conv_W_out).transpose(0, 2, 1).reshape(AREAS, CT, P, CHANNELS)
    a["b_out"] = np.asarray(L0_conv_b_out).reshape(AREAS, CT, P).transpose(0, 2, 1)
    a["gamma"] = np.asarray(L0_conv_gamma).reshape(CT, P).T
    a["beta"] = np.asarray(L0_conv_beta).reshape(CT, P).T
    a["ident"] = np.eye(P, dtype=np.float32)
    a = {k: np.ascontiguousarray(v) for k, v in a.items()}

    nc = bacc.Bacc("TRN2", target_bir_lowering=False, num_devices=1)
    ins = [nc.dram_tensor(f"in_{k}", a[k].shape, F32, kind="ExternalInput").ap() for k in _ORDER]
    out = nc.dram_tensor("out_y", (PAIRS, CT, P, TOKENS), F32, kind="ExternalOutput").ap()
    build(nc, *ins, out)
    r = run_bass_kernel_spmd(nc, [{f"in_{k}": a[k] for k in _ORDER}], core_ids=[0])
    got = np.asarray(r.results[0]["out_y"]).reshape(SPLIT, SPLIT, BATCH, CHANNELS, rows, cols)
    return np.ascontiguousarray(got.transpose(2, 3, 0, 4, 1, 5)).reshape(BATCH, CHANNELS, HEIGHT, WIDTH)
```

```python
from contextlib import ExitStack

import concourse.bass as bass
from concourse import mybir

F32 = mybir.dt.float32
F32R = mybir.dt.float32r
ALU = mybir.AluOpType
ACT = mybir.ActivationFunctionType

BATCH, CHANNELS, HEIGHT, WIDTH = 8, 256, 64, 64
SPLIT = 2
AREAS = SPLIT * SPLIT
HEADS = 8
DH = CHANNELS // HEADS
TOKENS = HEIGHT * WIDTH // AREAS
PAIRS = AREAS * BATCH
EPS = 1e-5
SCALE = float(DH) ** -0.5

P = 128
CT = CHANNELS // P
HALF = TOKENS // 2
HPS = 2
STEPS = HEADS // HPS
KEYS = TOKENS // P
SLOTS = STEPS * KEYS
LEAD = 2
GROUPS = 8
PRING = 4
QROWS = 3 * DH
CROWS = 2
ROWS = QROWS + CROWS
QUARTER = TOKENS // 4


class Pair:

    def __init__(self, reg, off):
        self.reg, self.off = reg, off

    def at(self, n, k):
        return self.off * n + k if self.reg is None else self.reg * (2 * n) + (self.off * n + k)

    def plus(self, k):
        return Pair(self.reg, self.off + k)

    def number(self):
        return self.off if self.reg is None else self.reg * 2 + self.off


LAST, CUR, NEXT = "last", "cur", "next"
FILL = [
    (0, 0, "bias", 0, LAST), (1, 2, "rowsum", 3, LAST), (3, 4, "v", 3, CUR), (5, 5, "outproj", 0, LAST),
    (6, 6, "maxrow", 1, CUR), (6, 7, "outproj", 1, LAST), (8, 8, "outproj", 2, LAST),
    (9, 10, "rowsum", 0, CUR), (11, 11, "outproj", 3, LAST), (12, 12, "qk", 0, NEXT),
    (13, 13, "mean", 0, LAST),
    (14, 14, "maxrow", 2, CUR), (14, 14, "qk", 1, NEXT), (15, 15, "qk", 2, NEXT), (16, 16, "qk", 3, NEXT),
    (17, 18, "rowsum", 1, CUR), (19, 20, "var", 0, LAST), (21, 21, "v", 0, NEXT),
    (22, 22, "maxrow", 3, CUR), (22, 23, "qk", 4, NEXT), (24, 24, "qk", 5, NEXT),
    (25, 26, "rowsum", 2, CUR), (27, 27, "qk", 6, NEXT), (28, 28, "qk", 7, NEXT), (29, 29, "v", 1, NEXT),
    (30, 30, "maxrow", 0, NEXT), (30, 31, "v", 2, NEXT),
]
NORMALISE = {0: 2, 1: 4, 2: 2, 3: 2}
CENTRE = {(15, 3): 0, (16, 3): 1, (18, 1): 2, (18, 3): 3}
SPREAD = (23, 2)
RESCALE = {(25, 3): 0, (26, 1): 1, (26, 3): 2, (29, 3): 3}
X_LOW = {(9, 1): 0, (9, 3): 1, (10, 1): 2, (10, 3): 3}
SQUARES, ROOT, AFFINE = {17: 0, 19: 1}, 22, {27: 0, 30: 1}
W_HIGH, X_HIGH = 7, {8: 0, 9: 1}


def fills(has):
    return [f for f in FILL if f[4] in has]


class Turn:

    def __init__(self, pair, parity, has):
        self.pair, self.parity, self.has = pair, parity, has
        self.fill = fills(has)

    def filled(self, kind, index):
        n = [(k, i) for _, _, k, i, _ in self.fill].index((kind, index))
        first = len(fills((NEXT,)))
        second = first + len(fills((CUR, NEXT)))
        full = len(FILL)
        if self.pair.reg is None:
            p = self.pair.off
            if p < 0:
                return n
            if p == 0:
                return first + n
            if p == PAIRS:
                return second + (PAIRS - 2) * full + len(fills((LAST, CUR))) + n
        return self.pair.at(full, second - full + n)

    def whose(self, name):
        return self.pair.plus({LAST: -1, CUR: 0, NEXT: 1}[name])


def turns(engine, emit):
    emit(Turn(Pair(None, -1), 1, (NEXT,)))
    emit(Turn(Pair(None, 0), 0, (CUR, NEXT)))
    with engine.Fori(0, PAIRS // 2 - 1) as i:
        emit(Turn(Pair(i, 1), 1, (LAST, CUR, NEXT)))
        emit(Turn(Pair(i, 2), 0, (LAST, CUR, NEXT)))
    emit(Turn(Pair(None, PAIRS - 1), 1, (LAST, CUR)))
    emit(Turn(Pair(None, PAIRS), 0, (LAST,)))


def max_groups(turn, u):
    v = u + LEAD
    step, group = v // KEYS + 1, v % KEYS
    pair, whose = (turn.pair, CUR) if step < STEPS else (turn.pair.plus(1), NEXT)
    return pair, step % STEPS, group, whose in turn.has


def build(nc, x, w_in, b_qk, b_v, w_out, b_out, gamma, beta, ident_in, out):
    with ExitStack() as ctx:
        def sb(name, shape, dt=F32):
            return ctx.enter_context(nc.sbuf_tensor(name, shape, dt))

        def sem(name):
            return ctx.enter_context(nc.semaphore(name))

        q_stack = sb("q_stack", [P, STEPS, HPS, TOKENS], F32R)
        k_stack = sb("k_stack", [P, STEPS, HPS, TOKENS], F32R)
        parts = sb("parts", [P, 2, 2, TOKENS], F32R)
        x_lo = sb("x_lo", [P, CT, TOKENS], F32R)
        x_hi = sb("x_hi", [P, CT, TOKENS], F32R)
        y = sb("y", [P, CT, TOKENS])
        v = sb("v", [P, 2, KEYS, CHANNELS])
        probs = sb("probs", [P, PRING, HPS * TOKENS])
        psum_of_p = sb("psum_of_p", [P, 2, HPS * TOKENS])
        attn = sb("attn", [P, CT, TOKENS])
        o_step = sb("o_step", [P, HALF])
        inv_sum = sb("inv_sum", [P, HALF])
        square = sb("square", [P, TOKENS])
        stat_q = sb("stat_q", [P, QUARTER])
        stat_all = sb("stat_all", [P, TOKENS])
        stat_t = sb("stat_t", [P, HALF])
        inv_col = sb("inv_col", [P, HALF // 32])
        var_col = sb("var_col", [P, QUARTER // 32])
        rstd_col = sb("rstd_col", [P, QUARTER // 32])
        w_lo = sb("w_lo", [P, CT, 3 * CHANNELS], F32R)
        w_hi = sb("w_hi", [P, CT, 3 * CHANNELS], F32R)
        x_whole = parts[:, 0, :, :].bitcast(F32)
        w_whole = parts[:, 1, :, :].rearrange("p t n -> p (t n)")[:, 0:3 * CT * CHANNELS].bitcast(F32)
        bqk = sb("bqk", [P, 2 * CT])
        wo = sb("wo", [P, CT, CHANNELS])
        bv = sb("bv", [P, CT])
        bo = sb("bo", [P, CT])
        bias = sb("bias", [P, CT])
        gb = sb("gb", [P, 2, CT])
        ident = sb("ident", [P, P])
        ones = sb("ones", [P, DH])
        mean_w = sb("mean_w", [P, DH])
        chunk_max = sb("chunk_max", [P, HPS * KEYS, 2])
        row_max = sb("row_max", [P, HPS * KEYS])
        neg_max = sb("neg_max", [P, CROWS, HPS * KEYS], F32R)
        max_rows = sb("max_rows", [CROWS * HPS * KEYS, P], F32R)

        ps_s = ctx.enter_context(nc.psum_tensor("ps_s", [P, HPS, TOKENS], F32))
        ps_m = ctx.enter_context(nc.psum_tensor("ps_m", [P, 2, HALF], F32))
        ps_o = ctx.enter_context(nc.psum_tensor("ps_o", [P, HALF], F32))
        ps_x = ctx.enter_context(nc.psum_tensor("ps_x", [P, HALF], F32))

        const_made = sem("const_made")
        const_loaded = sem("const_loaded")
        x_loaded = sem("x_loaded")
        w_hi_made = sem("w_hi_made")
        x_hi_made = sem("x_hi_made")
        w_lo_made = sem("w_lo_made")
        x_lo_made = sem("x_lo_made")
        wo_loaded = sem("wo_loaded")
        res_loaded = sem("res_loaded")
        built = [sem(f"built{s}") for s in range(STEPS)]
        crows_loaded = sem("crows_loaded")
        o_moved = sem("o_moved")
        out_stored = sem("out_stored")
        scores_done = sem("scores_done")
        exp_done = sem("exp_done")
        pv_done = sem("pv_done")
        chunk_done = sem("chunk_done")
        chunk_maxed = sem("chunk_maxed")
        max_split = sem("max_split")
        summed = sem("summed")
        x_filled = sem("x_filled")
        x_freed = sem("x_freed")
        qk_hi = sem("qk_hi")
        o_copied = sem("o_copied")
        o_normed = sem("o_normed")
        centred = sem("centred")
        sq_done = sem("sq_done")
        sq_used = sem("sq_used")
        inv_made = sem("inv_made")
        inv_spread = sem("inv_spread")
        var_read = sem("var_read")
        rstd_done = sem("rstd_done")
        rstd_spread = sem("rstd_spread")
        stat_loaded = sem("stat_loaded")
        sqrt_done = sem("sqrt_done")
        y_scaled = sem("y_scaled")
        y_final = sem("y_final")

        N_X, N_WO, N_RES, N_BUILT, N_CROWS, N_OMOVED = 48, 48, 16, 128, 16 * STEPS, 32 * STEPS
        N_STAT = 2 * 64
        N_S = N_E = 2 * SLOTS
        N_CHUNK = 4 * GROUPS * STEPS
        N_SPLIT, N_SUM = 3 * STEPS, (KEYS - 2) * STEPS

        block = ctx.enter_context(nc.Block())

        @block.sync
        def _(sp):
            def load_x(pair):
                n = pair.number()
                one = bass.ds(n, 1)
                area = bass.ds(n // BATCH, 1)
                sp.dma_start(w_whole.rearrange("p (t n) -> p t n", t=CT), w_in[area].rearrange("a t p n -> p (a t) n")
                             ).then_inc(x_loaded, 16)
                sp.dma_start(bqk[:, :], b_qk[area].rearrange("a p n -> (a p) n")).then_inc(x_loaded, 16)
                sp.dma_start(x_whole, x[one].rearrange("a t p n -> p (a t) n")).then_inc(x_loaded, 16)

            def build_stack(pair, step):
                for hh in range(HPS):
                    r = DH * ((step * HPS + hh) % 4)
                    q, k = (parts[r:r + DH, qk, :, :].bitcast(F32) for qk in range(2))
                    qs, ks = q_stack[:, step, hh, :].bitcast(F32), k_stack[:, step, hh, :].bitcast(F32)
                    sp.dma_start(qs[0:2 * DH], q).then_inc(built[step], 16)
                    sp.dma_start(ks[0:2 * DH], k[:, 0:1, :].broadcast_to([DH, 2, TOKENS])
                                 ).then_inc(built[step], 16)
                    sp.dma_start(qs[2 * DH:3 * DH], q[:, 0, :]).then_inc(built[step], 16)
                    sp.dma_start(ks[2 * DH:3 * DH], k[:, 1, :]).then_inc(built[step], 16)

            def load_crows(turn, pair, step, whose):
                sp.wait_ge(x_freed, turn.filled("maxrow", step) + 1)
                sp.dma_start(q_stack[QROWS:ROWS, step, :, :].bitcast(F32).rearrange("c h n -> c (h n)"),
                             max_rows[:, :].bitcast(F32)).then_inc(crows_loaded, 16)

            def move_o(turn, pair, step):
                sp.wait_ge(o_normed, pair.at(STEPS, step + 1))
                r = DH * ((step * HPS) % 4)
                for lh in range(2):
                    sp.dma_start(attn[r:r + HPS * DH, step // 2, lh * HALF:(lh + 1) * HALF],
                                 o_step[HPS * DH * lh:HPS * DH * (lh + 1), :]).then_inc(o_moved, 16)

            def spread_stat():
                for j in range(4):
                    sp.dma_start(stat_all[:, j * QUARTER:(j + 1) * QUARTER],
                                 stat_q[DH * j:DH * j + 1, :].unsqueeze(1).broadcast_to([1, P, QUARTER])
                                 ).then_inc(stat_loaded, 16)

            def load_wo(turn, pair):
                area = bass.ds((pair.number() // BATCH), 1)
                if LAST in turn.has:
                    sp.wait_ge(x_freed, turn.filled("outproj", 3) + 1)
                sp.dma_start(wo[:, :, :], w_out[area].rearrange("a t p n -> p (a t) n")).then_inc(wo_loaded, 16)
                sp.dma_start(bo[:, :], b_out[area].rearrange("a p n -> (a p) n")).then_inc(wo_loaded, 16)
                sp.dma_start(bv[:, :], b_v[area].rearrange("a p n -> (a p) n")).then_inc(wo_loaded, 16)

            sp.dma_start(ident[:, :], ident_in).then_inc(const_loaded, 16)
            sp.dma_start(gb[:, 0, :], gamma).then_inc(const_loaded, 16)
            sp.dma_start(gb[:, 1, :], beta).then_inc(const_loaded, 16)
            load_x(Pair(None, 0))

            def emit(turn):
                p, nxt, last = turn.pair, turn.pair.plus(1), turn.pair.plus(-1)
                if CUR in turn.has:
                    if LAST in turn.has:
                        sp.wait_ge(scores_done, p.at(N_S, 0))
                    build_stack(p, 3)
                if LAST in turn.has:
                    move_o(turn, last, 3)
                if CUR in turn.has:
                    if NEXT in turn.has:
                        sp.wait_ge(built[3], p.at(N_BUILT, N_BUILT))
                        load_x(nxt)
                    load_crows(turn, p, 1, CUR)
                    load_wo(turn, p)
                    move_o(turn, p, 0)
                if LAST in turn.has:
                    sp.wait_ge(x_freed, turn.filled("mean", 0) + 1)
                    spread_stat()
                if CUR in turn.has:
                    load_crows(turn, p, 2, CUR)
                if NEXT in turn.has:
                    sp.wait_ge(x_freed, turn.filled("qk", 3) + 1)
                    for step in range(2):
                        build_stack(nxt, step)
                if CUR in turn.has:
                    move_o(turn, p, 1)
                if CUR in turn.has:
                    load_crows(turn, p, 3, CUR)
                if LAST in turn.has:
                    sp.wait_ge(rstd_spread, last.at(1, 1))
                    spread_stat()
                if CUR in turn.has:
                    move_o(turn, p, 2)
                if NEXT in turn.has:
                    load_crows(turn, nxt, 0, NEXT)
                if LAST in turn.has:
                    n = (last.number())
                    sp.wait_ge(y_final, last.at(CT, CT))
                    sp.dma_start(out[bass.ds(n, 1)].rearrange("a t p n -> p (a t) n"),
                                 y[:, :, :]).then_inc(out_stored, 16)
                if NEXT in turn.has:
                    build_stack(nxt, 2)
                if CUR in turn.has:
                    n = (p.number())
                    if LAST in turn.has:
                        sp.wait_ge(out_stored, last.at(16, 16))
                    sp.dma_start(y[:, :, :], x[bass.ds(n, 1)].rearrange("a t p n -> p (a t) n")
                                 ).then_inc(res_loaded, 16)

            turns(sp, emit)
            sp.wait_ge(out_stored, 16 * PAIRS)

        @block.gpsimd
        def _(pool):
            pool.memset(ones[:, :], 1.0).then_inc(const_made, 1)
            pool.memset(mean_w[:, :], 1.0 / CHANNELS).then_inc(const_made, 1)

            def low_weights(pair):
                pool.wait_ge(w_hi_made, pair.at(1, 1))
                lo, hi = (w[:, :, :].rearrange("p t n -> p (t n)") for w in (w_lo, w_hi))
                pool.tensor_tensor(lo, w_whole, hi.bitcast(F32),
                                   ALU.subtract).then_inc(w_lo_made, 1)

            def emit(turn):
                p = turn.pair
                if CUR not in turn.has:
                    if NEXT in turn.has:
                        low_weights(p.plus(1))
                    return
                for s in range(STEPS):
                    if s == 1 and NEXT in turn.has:
                        low_weights(p.plus(1))
                    acc = psum_of_p[:, s % 2, :]
                    if s >= 2:
                        pool.wait_ge(x_freed, turn.filled("rowsum", s - 2) + 1)
                    elif LAST in turn.has:
                        pool.wait_ge(pv_done, p.at(SLOTS, 0))
                        if s == 1:
                            pool.wait_ge(x_freed, turn.filled("rowsum", 3) + 1)
                        else:
                            pool.wait_ge(x_freed, turn.filled("rowsum", 3))
                    for t in range(1, KEYS - 1):
                        u = s * KEYS + t
                        pool.wait_ge(exp_done, p.at(N_E, 2 * (u + 1)))
                        first = probs[:, (u - 1) % PRING, :] if t == 1 else acc
                        if t > 1:
                            pool.wait_ge(summed, p.at(N_SUM, s * (KEYS - 2) + t - 1))
                        pool.tensor_tensor(acc, first, probs[:, u % PRING, :], ALU.add).then_inc(summed, 1)

            turns(pool, emit)

        @block.scalar
        def _(act):
            def fill_copies(turn, u):
                for _, slot, kind, i, whose in turn.fill:
                    if slot != u:
                        continue
                    n = turn.filled(kind, i)
                    pair = turn.whose(whose)
                    if kind == "qk":
                        m, half = i // 2, i % 2
                        hi = parts[:, m % 2, 0, half * HALF:(half + 1) * HALF]
                        act.wait_ge(x_filled, n + 1)
                        if i >= 4:
                            act.wait_ge(built[0], pair.at(N_BUILT, N_BUILT))
                            act.wait_ge(built[1], pair.at(N_BUILT, N_BUILT))
                        elif CUR in turn.has:
                            act.wait_ge(built[2], pair.at(N_BUILT, 0))
                            act.wait_ge(built[3], pair.at(N_BUILT, 0))
                        act.activation(hi, ps_x[:, :], ACT.Identity, bias=bqk[:, m:m + 1]).then_inc(qk_hi, 1)
                    elif kind == "v":
                        par = turn.parity if whose == CUR else 1 - turn.parity
                        act.wait_ge(x_filled, n + 1)
                        act.activation(v[:, par, 2 * i:2 * i + 2, :].rearrange("p a b -> p (a b)"), ps_x[:, :],
                                       ACT.Copy).then_inc(x_freed, 1)
                    elif kind == "mean":
                        act.wait_ge(x_filled, n + 1)
                        act.activation(stat_q[:, :], ps_x[:, 0:QUARTER], ACT.Copy).then_inc(x_freed, 1)

            def copy_maxrow(turn, u):
                for slot, _, kind, i, whose in turn.fill:
                    if slot == u and kind == "maxrow":
                        act.wait_ge(x_filled, turn.filled(kind, i) + 1)
                        if not (turn.pair.reg is None and turn.pair.off < 0):
                            act.wait_ge(crows_loaded, turn.whose(whose).at(N_CROWS, 16 * i))
                        act.activation(max_rows[:, :], ps_x[0:CROWS * HPS * KEYS, 0:P], ACT.Copy
                                       ).then_inc(x_freed, 1)

            def emit(turn):
                p, last = turn.pair, turn.pair.plus(-1)
                for u in range(SLOTS):
                    if CUR not in turn.has:
                        copy_maxrow(turn, u)
                    if CUR in turn.has:
                        for hh in range(HPS):
                            if hh == 1:
                                copy_maxrow(turn, u)
                            act.wait_ge(scores_done, p.at(N_S, 2 * u + hh + 1))
                            if u >= PRING or LAST in turn.has:
                                b = u - PRING
                                bs, bt = b // KEYS, b % KEYS
                                act.wait_ge(pv_done, p.at(SLOTS, b + 1))
                                if bt == KEYS - 1:
                                    act.wait_ge(x_filled, turn.filled("rowsum", bs % STEPS) + 1)
                                else:
                                    act.wait_ge(summed, p.at(N_SUM, bs * (KEYS - 2) + max(bt, 1)))
                            act.activation(probs[:, u % PRING, hh * TOKENS:(hh + 1) * TOKENS],
                                           ps_s[:, hh, :], ACT.Exp, scale=SCALE).then_inc(exp_done, 1)
                    if u % KEYS == 0 and ((u > 0 and CUR in turn.has) or (u == 0 and LAST in turn.has)):
                        act.wait_ge(pv_done, p.at(SLOTS, u))
                        s = u // KEYS
                        if not (turn.pair.reg is None and turn.pair.off == 0 and s == 1):
                            act.wait_ge(o_moved, p.at(N_OMOVED, 32 * (s - 1)))
                        act.activation(o_step[:, :], ps_o[:, :], ACT.Copy).then_inc(o_copied, 1)
                    if NEXT in turn.has and u == W_HIGH:
                        act.wait_ge(x_loaded, p.plus(1).at(N_X, N_X))
                        act.activation(w_hi[:, :, :].rearrange("p t n -> p (t n)"),
                                       w_whole, ACT.Copy).then_inc(w_hi_made, 1)
                    if NEXT in turn.has and u in X_HIGH:
                        t = X_HIGH[u]
                        act.activation(x_hi[:, t, :], x_whole[:, t, :], ACT.Copy).then_inc(x_hi_made, 1)
                    if LAST in turn.has and u in SQUARES:
                        m = SQUARES[u]
                        act.wait_ge(centred, last.at(2 * CT, 2 * m + 2))
                        if m > 0:
                            act.wait_ge(sq_used, last.at(1, m))
                        act.activation(square[:, :], y[:, m, :], ACT.Square).then_inc(sq_done, 1)
                    if LAST in turn.has and u == ROOT:
                        act.wait_ge(rstd_done, last.at(1, 1))
                        act.activation(rstd_col[:, :], rstd_col[:, :], ACT.Sqrt).then_inc(sqrt_done, 1)
                    if LAST in turn.has and u in AFFINE:
                        m = AFFINE[u]
                        act.wait_ge(y_scaled, last.at(2 * CT, 2 * m + 2))
                        act.activation(y[:, m, :], y[:, m, :], ACT.Identity, bias=gb[:, 1, m:m + 1],
                                       scale=gb[:, 0, m:m + 1]).then_inc(y_final, 1)
                    fill_copies(turn, u)

            act.wait_ge(const_loaded, 48)
            turns(act, emit)

        @block.vector
        def _(dve):
            def spread(col):
                return col.unsqueeze(2).broadcast_to([P, col.shape[1], 32])

            def after_fill(turn, u, place):
                for _, slot, kind, i, whose in turn.fill:
                    n = turn.filled(kind, i)
                    pair = turn.whose(whose)
                    if kind == "rowsum" and u + 1 == slot + NORMALISE[i] and place == 0:
                        dve.wait_ge(inv_spread, pair.at(STEPS, i + 1))
                        dve.wait_ge(o_copied, pair.at(STEPS, i + 1))
                        dve.tensor_tensor(o_step[:, :], o_step[:, :], inv_sum[:, :], ALU.mult).then_inc(o_normed, 1)
                    if slot != u:
                        continue
                    if kind == "rowsum":
                        if place == 0:
                            dve.wait_ge(x_filled, n + 1)
                            dve.transpose(stat_t[:, :], ps_x[:, :]).then_inc(x_freed, 1)
                        elif place == 1:
                            dve.wait_ge(x_freed, n + 1)
                            dve.reciprocal(inv_col[:, :], stat_t[:, 0:HALF:32]).then_inc(inv_made, 1)
                        elif place == 3:
                            dve.wait_ge(inv_made, pair.at(STEPS, i + 1))
                            dve.transpose(inv_sum[:, :], spread(inv_col[:, :])).then_inc(inv_spread, 1)
                    elif kind == "qk" and place == 1:
                        m, half = i // 2, i % 2
                        hi, lo = (parts[:, m % 2, j, half * HALF:(half + 1) * HALF] for j in range(2))
                        dve.wait_ge(qk_hi, pair.at(8, i + 1))
                        dve.scalar_tensor_tensor(out=lo, in0=ps_x[:, :], scalar=bqk[:, m:m + 1],
                                                 in1=hi.bitcast(F32), op0=ALU.add, op1=ALU.subtract
                                                 ).then_inc(x_freed, 1)
                    elif kind == "bias" and place == 0:
                        dve.wait_ge(x_filled, n + 1)
                        dve.tensor_tensor(bias[:, :], ps_x[:, 0:CT], bo[:, :], ALU.add).then_inc(x_freed, 1)
                    elif kind == "outproj" and place == 0:
                        half, m = i // 2, i % 2
                        dve.wait_ge(x_filled, n + 1)
                        dve.wait_ge(res_loaded, pair.at(N_RES, N_RES))
                        t = y[:, m, half * HALF:(half + 1) * HALF]
                        dve.scalar_tensor_tensor(out=t, in0=ps_x[:, :], scalar=bias[:, m:m + 1], in1=t,
                                                 op0=ALU.add, op1=ALU.add).then_inc(x_freed, 1)
                    elif kind == "var":
                        if place == 0:
                            dve.wait_ge(x_filled, n + 1)
                            dve.transpose(stat_t[:, 0:QUARTER], ps_x[:, 0:QUARTER]).then_inc(x_freed, 1)
                        elif place == 1:
                            dve.wait_ge(x_freed, n + 1)
                            dve.tensor_scalar(var_col[:, :], stat_t[:, 0:QUARTER:32], EPS, None, ALU.add
                                              ).then_inc(var_read, 1)
                        elif place == 2:
                            dve.wait_ge(var_read, pair.at(1, 1))
                            dve.reciprocal(rstd_col[:, :], var_col[:, :]).then_inc(rstd_done, 1)

            def emit(turn):
                last = turn.pair.plus(-1)
                for u in range(SLOTS):
                    pair, step, group, exists = max_groups(turn, u)
                    for i in range(4):
                        after_fill(turn, u - 1, i)
                        if NEXT in turn.has and (u, i) in X_LOW:
                            t, half = X_LOW[u, i] // 2, X_LOW[u, i] % 2
                            cols = slice(half * HALF, (half + 1) * HALF)
                            dve.wait_ge(x_hi_made, turn.pair.plus(1).at(CT, t + 1))
                            dve.tensor_tensor(x_lo[:, t, cols], x_whole[:, t, cols],
                                              x_hi[:, t, cols].bitcast(F32), ALU.subtract).then_inc(x_lo_made, 1)
                        if LAST in turn.has and (u, i) in CENTRE:
                            m, half = CENTRE[u, i] // 2, CENTRE[u, i] % 2
                            cols = slice(half * HALF, (half + 1) * HALF)
                            dve.wait_ge(stat_loaded, last.at(N_STAT, N_STAT // 2))
                            dve.tensor_tensor(y[:, m, cols], y[:, m, cols], stat_all[:, cols], ALU.subtract
                                              ).then_inc(centred, 1)
                        if LAST in turn.has and (u, i) == SPREAD:
                            dve.wait_ge(sqrt_done, last.at(1, 1))
                            dve.transpose(stat_q[:, :], spread(rstd_col[:, :])).then_inc(rstd_spread, 1)
                        if LAST in turn.has and (u, i) in RESCALE:
                            m, half = RESCALE[u, i] // 2, RESCALE[u, i] % 2
                            cols = slice(half * HALF, (half + 1) * HALF)
                            dve.wait_ge(stat_loaded, last.at(N_STAT, N_STAT))
                            dve.tensor_tensor(y[:, m, cols], y[:, m, cols], stat_all[:, cols], ALU.mult
                                              ).then_inc(y_scaled, 1)
                        if exists:
                            c = 4 * group + i
                            col = chunk_max[:, c // 2, c % 2:c % 2 + 1]
                            k = step * 4 * GROUPS + c
                            dve.wait_ge(chunk_done, pair.at(N_CHUNK, k + 1))
                            dve.tensor_reduce(col, ps_m[:, c % 2, :], mybir.AxisListType.X, ALU.max
                                              ).then_inc(chunk_maxed, 1)
                    if exists:
                        if group == GROUPS - 1:
                            k = step * 3
                            dve.wait_ge(chunk_maxed, pair.at(N_CHUNK, (step + 1) * 4 * GROUPS))
                            dve.tensor_tensor(row_max[:, :], chunk_max[:, :, 0], chunk_max[:, :, 1],
                                              ALU.max).then_inc(max_split, 1)
                            dve.wait_ge(max_split, pair.at(N_SPLIT, k + 1))
                            if not (pair.reg is None and pair.off == 0 and step == 0):
                                dve.wait_ge(crows_loaded, pair.at(N_CROWS, 16 * step))
                            dve.tensor_scalar(neg_max[:, 0, :], row_max[:, :], -1.0, None, ALU.mult
                                              ).then_inc(max_split, 1)
                            dve.wait_ge(max_split, pair.at(N_SPLIT, k + 2))
                            dve.scalar_tensor_tensor(out=neg_max[:, 1, :], in0=row_max[:, :], scalar=-1.0,
                                                     in1=neg_max[:, 0, :].bitcast(F32), op0=ALU.mult,
                                                     op1=ALU.subtract).then_inc(max_split, 1)

            dve.memset(k_stack[QROWS:ROWS, :, :, :].bitcast(F32), 1.0).then_inc(const_made, 1)
            turns(dve, emit)

        @block.tensor
        def _(pe):
            pe.wait_ge(const_loaded, 48)
            pe.wait_ge(const_made, 3)
            TERMS = ((w_hi, x_hi), (w_hi, x_lo), (w_lo, x_hi))

            def scores(turn, u, hh):
                p, s, t = turn.pair, u // KEYS, u % KEYS
                if hh == 0 and t == 0:
                    pe.wait_ge(crows_loaded, p.at(N_CROWS, 16 * (s + 1)))
                if u > 0 or LAST in turn.has:
                    pe.wait_ge(exp_done, p.at(N_E, 2 * (u - 1) + hh + 1))
                for lh in range(2):
                    ins = pe.matmul(ps_s[:, hh, lh * HALF:(lh + 1) * HALF],
                                    k_stack[0:ROWS, s, hh, t * P:(t + 1) * P],
                                    q_stack[0:ROWS, s, hh, lh * HALF:(lh + 1) * HALF], start=True, stop=True)
                ins.then_inc(scores_done, 1)

            def max_chunks(turn, u, which):
                pair, step, group, exists = max_groups(turn, u)
                if not exists:
                    return
                if group == 0 and 0 in which:
                    pe.wait_ge(built[step], pair.at(N_BUILT, N_BUILT))
                for i in which:
                    c = 4 * group + i
                    hh, lt, mh = c // (2 * KEYS), c // 2 % KEYS, c % 2
                    k = step * 4 * GROUPS + c
                    if k >= 2 or not (pair.reg is None and pair.off == 0):
                        pe.wait_ge(chunk_maxed, pair.at(N_CHUNK, k - 1))
                    pe.matmul(ps_m[:, c % 2, :], q_stack[0:QROWS, step, hh, lt * P:(lt + 1) * P],
                              k_stack[0:QROWS, step, hh, mh * HALF:(mh + 1) * HALF],
                              start=True, stop=True).then_inc(chunk_done, 1)

            def weighted(pair, parity, u):
                s, t = u // KEYS, u % KEYS
                pe.wait_ge(exp_done, pair.at(N_E, 2 * (u + 1)))
                if t == 0 and not (pair.reg is None and pair.off == 0 and s == 0):
                    pe.wait_ge(o_copied, pair.at(STEPS, s))
                for lh in range(2):
                    for hh in range(HPS):
                        j, h = HPS * lh + hh, s * HPS + hh
                        ins = pe.matmul(ps_o[DH * j:DH * (j + 1), :], v[:, parity, t, h * DH:(h + 1) * DH],
                                        probs[:, u % PRING, (2 * hh + lh) * HALF:(2 * hh + lh + 1) * HALF],
                                        start=(t == 0), stop=(t == KEYS - 1), tile_position=(0, DH * j))
                ins.then_inc(pv_done, 1)

            def fill(turn, kind, i, whose, part):
                n = turn.filled(kind, i)
                pair = turn.whose(whose)
                if part == 0 and not (turn.pair.reg is None and turn.pair.off < 0 and n == 0):
                    pe.wait_ge(x_freed, n)
                first, last = part == 0, part == 1
                if kind == "rowsum":
                    if part == 0:
                        src = probs[:, (KEYS * (i + 1) - 1) % PRING, :]
                    else:
                        pe.wait_ge(summed, pair.at(N_SUM, (i + 1) * (KEYS - 2)))
                        src = psum_of_p[:, i % 2, :]
                    for j in range(4):
                        c = 2 * (j % HPS) + j // HPS
                        ins = pe.matmul(ps_x[DH * j:DH * (j + 1), :], ones[:, :], src[:, c * HALF:(c + 1) * HALF],
                                        start=first, stop=last, tile_position=(0, DH * j))
                elif kind == "bias":
                    if part == 1:
                        return
                    pe.wait_ge(wo_loaded, pair.at(N_WO, N_WO))
                    for m in range(CT):
                        for t in range(CT):
                            ins = pe.matmul(ps_x[:, m:m + 1], wo[:, t, m * P:(m + 1) * P], bv[:, t:t + 1],
                                            start=(t == 0), stop=(t == CT - 1))
                elif kind == "outproj":
                    half, m = i // 2, i % 2
                    if part == 0:
                        pe.wait_ge(o_moved, pair.at(N_OMOVED, N_OMOVED))
                    ins = pe.matmul(ps_x[:, :], wo[:, part, m * P:(m + 1) * P],
                                    attn[:, part, half * HALF:(half + 1) * HALF], start=first, stop=last)
                elif kind in ("mean", "var"):
                    if kind == "var":
                        pe.wait_ge(sq_done, pair.at(CT, part + 1))
                    src = y[:, part, :] if kind == "mean" else square[:, :]
                    for j in range(4):
                        ins = pe.matmul(ps_x[DH * j:DH * (j + 1), 0:QUARTER], mean_w[:, :],
                                        src[:, j * QUARTER:(j + 1) * QUARTER],
                                        start=first, stop=last, tile_position=(0, DH * j))
                    if kind == "var" and not last:
                        ins.then_inc(sq_used, 1)
                elif kind == "qk":
                    m, half = i // 2, i % 2
                    col = (m % 2) * CHANNELS + (m // 2) * P
                    pe.wait_ge(x_lo_made, pair.at(2 * CT, 2 * CT))
                    pe.wait_ge(w_lo_made, pair.at(1, 1))
                    for j, (wt, xt) in enumerate(TERMS):
                        ins = pe.matmul(ps_x[:, :], wt[:, part, col:col + P],
                                        xt[:, part, half * HALF:(half + 1) * HALF],
                                        start=first and j == 0, stop=last and j == len(TERMS) - 1)
                elif kind == "v":
                    kt = 2 * i + part
                    n_terms = CT * len(TERMS)
                    for j in range(n_terms):
                        t, (wt, xt) = j // len(TERMS), TERMS[j % len(TERMS)]
                        ins = pe.matmul(ps_x[:, part * CHANNELS:(part + 1) * CHANNELS],
                                        xt[:, t, kt * P:(kt + 1) * P], wt[:, t, 2 * CHANNELS:3 * CHANNELS],
                                        start=(j == 0), stop=(j == n_terms - 1))
                elif kind == "maxrow":
                    pe.wait_ge(max_split, pair.at(N_SPLIT, 3 * (i + 1)))
                    ins = pe.transpose(ps_x[0:CROWS * HPS * KEYS, 0:P],
                                       neg_max[:, :, :].rearrange("p a b -> p (a b)").bitcast(F32), ident[:, :])
                if last or kind in ("maxrow", "bias"):
                    ins.then_inc(x_filled, 1)

            def emit(turn):
                p = turn.pair
                for u in range(SLOTS):
                    if CUR in turn.has:
                        scores(turn, u, 0)
                    max_chunks(turn, u, (0,))
                    if u > 0 and CUR in turn.has:
                        weighted(p, turn.parity, u - 1)
                    elif u == 0 and LAST in turn.has:
                        weighted(p.plus(-1), 1 - turn.parity, SLOTS - 1)
                    max_chunks(turn, u, (1,))
                    for slot, _, kind, i, whose in turn.fill:
                        if slot == u and kind == "maxrow":
                            fill(turn, kind, i, whose, 0)
                    if CUR in turn.has:
                        scores(turn, u, 1)
                    max_chunks(turn, u, (2,))
                    now = [(kind, i, whose, part) for *slots, kind, i, whose in turn.fill for part in range(2)
                           if slots[part] == u and kind != "maxrow"]
                    for f in now[:1]:
                        fill(turn, *f)
                    max_chunks(turn, u, (3,))
                    for f in now[1:]:
                        fill(turn, *f)

            turns(pe, emit)


_ORDER = ("x", "w_in", "b_qk", "b_v", "w_out", "b_out", "gamma", "beta", "ident")


def kernel(x, L0_conv_W_in, L0_conv_b_in, L0_conv_W_out, L0_conv_b_out, L0_conv_gamma, L0_conv_beta):
    import numpy as np
    import concourse.bacc as bacc
    from concourse.bass_utils import run_bass_kernel_spmd

    rows, cols = HEIGHT // SPLIT, WIDTH // SPLIT
    a = {}
    t = np.asarray(x).reshape(BATCH, CHANNELS, SPLIT, rows, SPLIT, cols).transpose(2, 4, 0, 1, 3, 5)
    a["x"] = t.reshape(PAIRS, CT, P, TOKENS)
    a["w_in"] = np.asarray(L0_conv_W_in).transpose(0, 2, 1).reshape(AREAS, CT, P, 3 * CHANNELS)
    b_in = np.asarray(L0_conv_b_in)
    a["b_qk"] = b_in[:, :2 * CHANNELS].reshape(AREAS, 2, CT, P).transpose(0, 3, 2, 1).reshape(AREAS, P, 2 * CT)
    a["b_v"] = b_in[:, 2 * CHANNELS:].reshape(AREAS, CT, P).transpose(0, 2, 1)
    a["w_out"] = np.asarray(L0_conv_W_out).transpose(0, 2, 1).reshape(AREAS, CT, P, CHANNELS)
    a["b_out"] = np.asarray(L0_conv_b_out).reshape(AREAS, CT, P).transpose(0, 2, 1)
    a["gamma"] = np.asarray(L0_conv_gamma).reshape(CT, P).T
    a["beta"] = np.asarray(L0_conv_beta).reshape(CT, P).T
    a["ident"] = np.eye(P, dtype=np.float32)
    a = {k: np.ascontiguousarray(v) for k, v in a.items()}

    nc = bacc.Bacc("TRN2", target_bir_lowering=False, num_devices=1)
    ins = [nc.dram_tensor(f"in_{k}", a[k].shape, F32, kind="ExternalInput").ap() for k in _ORDER]
    out = nc.dram_tensor("out_y", (PAIRS, CT, P, TOKENS), F32, kind="ExternalOutput").ap()
    build(nc, *ins, out)
    r = run_bass_kernel_spmd(nc, [{f"in_{k}": a[k] for k in _ORDER}], core_ids=[0])
    got = np.asarray(r.results[0]["out_y"]).reshape(SPLIT, SPLIT, BATCH, CHANNELS, rows, cols)
    return np.ascontiguousarray(got.transpose(2, 3, 0, 4, 1, 5)).reshape(BATCH, CHANNELS, HEIGHT, WIDTH)
```
